# Optimizing a Trainium2 kernel written in Bass

```python
import numpy as np
import jax
import jax.numpy as jnp

def _softmax(x, axis=-1):
    return jax.nn.softmax(x, axis=axis)

def _gelu(x):
    return jax.nn.gelu(x, approximate=True)

def _silu(x):
    return jax.nn.silu(x)

def _sigmoid(x):
    return jax.nn.sigmoid(x)

def _layernorm(x, axis=-1, eps=1e-05):
    m = jnp.mean(x, axis=axis, keepdims=True)
    v = jnp.var(x, axis=axis, keepdims=True)
    return (x - m) / jnp.sqrt(v + eps)

def _scatter_add(tgt, idx, src, axis=0):
    return tgt.at[idx].add(src)

def _segment_sum(src, seg, n):
    return jax.ops.segment_sum(src, seg, n)
kernel_name = 'mk_decoder_preln_d1_seqx_r4_0e44dd'

def setup_inputs(seed: int=0):
    np.random.seed(seed)
    _w = jnp.asarray

    def _rec_inputs():
        import jax
        import jax.numpy as jnp
        _rk = jax.random.key(seed)
        x = 7.22e-05 + 1 * jax.random.normal(jax.random.fold_in(_rk, 1), (4, 512, 256), jnp.float32)
        _lenS = 512 - jax.random.randint(jax.random.fold_in(_rk, 7), (4,), 0, max(1, 512 // 4) + 1, jnp.int32)
        _lenS2 = 512 - jax.random.randint(jax.random.fold_in(_rk, 8), (4,), 0, max(1, 512 // 4) + 1, jnp.int32)
        _ctx_768P = jax.random.normal(jax.random.fold_in(_rk, 11), (4, 16, 192), jnp.float32)
        _ctx_768c = jax.random.dirichlet(jax.random.fold_in(_rk, 511), 0.3 * jnp.ones((16,), jnp.float32), (4, 512))
        _ctx_768t = jnp.einsum('bsk,bkd->bsd', _ctx_768c, _ctx_768P)
        _ctx_768t = _ctx_768t * jax.lax.rsqrt(jnp.mean(jnp.square(_ctx_768t)) + 1e-12) * 0.953939
        ctx_768 = 2.09791e-05 + 1.00001 * (_ctx_768t + 0.3 * jax.random.normal(jax.random.fold_in(_rk, 611), (4, 512, 192), jnp.float32))
        return (x, ctx_768)
    x, ctx_768 = _rec_inputs()

    def _L0_attn_setup():
        import jax, jax.numpy as jnp
        import numpy as np
        B, S, D = (2, 512, 256)
        N_HEADS = 16
        HEAD_DIM = D // N_HEADS
        THETA = 10000.0

        def rope_tables(seq, head_dim, dtype=jnp.float32):
            half = head_dim // 2
            freqs = 1.0 / THETA ** (jnp.arange(half, dtype=jnp.float32) / half)
            angles = jnp.arange(seq, dtype=jnp.float32)[:, None] * freqs[None, :]
            return (jnp.cos(angles).astype(dtype), jnp.sin(angles).astype(dtype))

        def apply_rope_interleaved(x, cos, sin):
            x_even = x[..., 0::2]
            x_odd = x[..., 1::2]
            r_even = x_even * cos - x_odd * sin
            r_odd = x_even * sin + x_odd * cos
            out = jnp.stack([r_even, r_odd], axis=-1).reshape(x.shape)
            return out
        key = jax.random.key(seed)
        ks = jax.random.split(key, 6)
        scale = 1.0 / np.sqrt(D)
        return {'x': jax.random.normal(ks[0], (B, S, D), dtype=jnp.float32), 'Wq': jax.random.normal(ks[1], (D, D), dtype=jnp.float32) * scale, 'Wk': jax.random.normal(ks[2], (D, D), dtype=jnp.float32) * scale, 'Wv': jax.random.normal(ks[3], (D, D), dtype=jnp.float32) * scale, 'Wo': jax.random.normal(ks[4], (D, D), dtype=jnp.float32) * scale, 'bo': jnp.zeros((D,), dtype=jnp.float32)}
    _L0_attn_all = _L0_attn_setup()
    _L0_attn_in = {k: v for k, v in _L0_attn_all.items() if k in ('Wq', 'Wk', 'Wv', 'Wo', 'bo')}
    del _L0_attn_all

    def _L0_xattn_setup():
        import jax, jax.numpy as jnp
        import numpy as np
        N_HEAD = 16
        D_EMBED = 256
        D_CROSS = 192
        D_HEAD = D_EMBED // N_HEAD
        key = jax.random.key(seed)
        ks = jax.random.split(key, 8)
        B, SQ, SKV = (2, 1024, 512)
        s_q = 1.0 / np.sqrt(D_EMBED)
        s_kv = 1.0 / np.sqrt(D_CROSS)
        return {'x': jax.random.normal(ks[0], (B, SQ, D_EMBED), jnp.float32), 'y': jax.random.normal(ks[1], (B, SKV, D_CROSS), jnp.float32), 'Wq': jax.random.normal(ks[2], (D_EMBED, D_EMBED), jnp.float32) * s_q, 'bq': jnp.zeros((D_EMBED,), jnp.float32), 'Wkv': jax.random.normal(ks[3], (D_CROSS, 2 * D_EMBED), jnp.float32) * s_kv, 'bkv': jnp.zeros((2 * D_EMBED,), jnp.float32), 'Wo': jax.random.normal(ks[4], (D_EMBED, D_EMBED), jnp.float32) * s_q, 'bo': jnp.zeros((D_EMBED,), jnp.float32)}
    _L0_xattn_all = _L0_xattn_setup()
    _L0_xattn_in = {k: v for k, v in _L0_xattn_all.items() if k in ('Wq', 'bq', 'Wkv', 'bkv', 'Wo', 'bo')}
    del _L0_xattn_all

    def _L0_ffn_setup():
        import jax, jax.numpy as jnp
        import numpy as np
        B, L, H, E, I = (4, 512, 256, 8, 1024)
        S = B * L
        CAP_FACTOR_EVAL = 2.0
        MIN_CAP = 4
        _cap = int(np.floor(CAP_FACTOR_EVAL * S / E))
        _cap += _cap % 2
        CAPACITY = max(_cap, MIN_CAP)

        def _layer_norm(x, g, b, eps=1e-05):
            mu = x.mean(-1, keepdims=True)
            var = ((x - mu) ** 2).mean(-1, keepdims=True)
            return (x - mu) * jax.lax.rsqrt(var + eps) * g + b
        key = jax.random.key(seed)
        ks = jax.random.split(key, 8)
        gate_std = float(np.sqrt(0.1 / H))
        return {'inputs': jax.random.normal(ks[0], (B, L, H), jnp.float32), 'gate_weight': jax.random.normal(ks[1], (E, H), jnp.float32) * gate_std, 'ln_gamma': jnp.ones((H,), jnp.float32), 'ln_beta': jnp.zeros((H,), jnp.float32), 'wi': jax.random.normal(ks[2], (E, H, I), jnp.float32) * float(1.0 / np.sqrt(H)), 'wo': jax.random.normal(ks[3], (E, I, H), jnp.float32) * float(1.0 / np.sqrt(I)), 'conf_w1': jax.random.normal(ks[4], (H // 2, H), jnp.float32) * float(np.sqrt(2.0 / (H + H // 2))), 'conf_b1': -jnp.ones((H // 2,), jnp.float32), 'conf_w2': jax.random.normal(ks[5], (1, H // 2), jnp.float32) * float(np.sqrt(2.0 / (1 + H // 2))), 'conf_b2': -jnp.ones((1,), jnp.float32), 'comp_w': jax.random.normal(ks[6], (1, H), jnp.float32) * float(1.0 / np.sqrt(H)), 'comp_b': jnp.zeros((1,), jnp.float32)}
    _L0_ffn_all = _L0_ffn_setup()
    _L0_ffn_in = {k: v for k, v in _L0_ffn_all.items() if k in ('gate_weight', 'ln_gamma', 'ln_beta', 'wi', 'wo', 'conf_w1', 'conf_b1', 'conf_w2', 'conf_b2', 'comp_w', 'comp_b')}
    del _L0_ffn_all
    return {'x': x, 'ctx_768': ctx_768, 'L0_attn_Wq': _L0_attn_in['Wq'], 'L0_attn_Wk': _L0_attn_in['Wk'], 'L0_attn_Wv': _L0_attn_in['Wv'], 'L0_attn_Wo': _L0_attn_in['Wo'], 'L0_attn_bo': _L0_attn_in['bo'], 'L0_xattn_Wq': _L0_xattn_in['Wq'], 'L0_xattn_bq': _L0_xattn_in['bq'], 'L0_xattn_Wkv': _L0_xattn_in['Wkv'], 'L0_xattn_bkv': _L0_xattn_in['bkv'], 'L0_xattn_Wo': _L0_xattn_in['Wo'], 'L0_xattn_bo': _L0_xattn_in['bo'], 'L0_ffn_gate_weight': _L0_ffn_in['gate_weight'], 'L0_ffn_ln_gamma': _L0_ffn_in['ln_gamma'], 'L0_ffn_ln_beta': _L0_ffn_in['ln_beta'], 'L0_ffn_wi': _L0_ffn_in['wi'], 'L0_ffn_wo': _L0_ffn_in['wo'], 'L0_ffn_conf_w1': _L0_ffn_in['conf_w1'], 'L0_ffn_conf_b1': _L0_ffn_in['conf_b1'], 'L0_ffn_conf_w2': _L0_ffn_in['conf_w2'], 'L0_ffn_conf_b2': _L0_ffn_in['conf_b2'], 'L0_ffn_comp_w': _L0_ffn_in['comp_w'], 'L0_ffn_comp_b': _L0_ffn_in['comp_b']}

def reference(x, ctx_768, L0_attn_Wq, L0_attn_Wk, L0_attn_Wv, L0_attn_Wo, L0_attn_bo, L0_xattn_Wq, L0_xattn_bq, L0_xattn_Wkv, L0_xattn_bkv, L0_xattn_Wo, L0_xattn_bo, L0_ffn_gate_weight, L0_ffn_ln_gamma, L0_ffn_ln_beta, L0_ffn_wi, L0_ffn_wo, L0_ffn_conf_w1, L0_ffn_conf_b1, L0_ffn_conf_w2, L0_ffn_conf_b2, L0_ffn_comp_w, L0_ffn_comp_b):
    import jax
    import jax.numpy as jnp

    def _L0_attn_ref(x, Wq, Wk, Wv, Wo, bo):
        import jax, jax.numpy as jnp
        import numpy as np
        B, S, D = (2, 512, 256)
        N_HEADS = 16
        HEAD_DIM = D // N_HEADS
        THETA = 10000.0

        def rope_tables(seq, head_dim, dtype=jnp.float32):
            half = head_dim // 2
            freqs = 1.0 / THETA ** (jnp.arange(half, dtype=jnp.float32) / half)
            angles = jnp.arange(seq, dtype=jnp.float32)[:, None] * freqs[None, :]
            return (jnp.cos(angles).astype(dtype), jnp.sin(angles).astype(dtype))

        def apply_rope_interleaved(x, cos, sin):
            x_even = x[..., 0::2]
            x_odd = x[..., 1::2]
            r_even = x_even * cos - x_odd * sin
            r_odd = x_even * sin + x_odd * cos
            out = jnp.stack([r_even, r_odd], axis=-1).reshape(x.shape)
            return out
        b, s, _ = x.shape

        def proj(W):
            return jnp.einsum('bsd,de->bse', x, W).reshape(b, s, N_HEADS, HEAD_DIM).transpose(0, 2, 1, 3)
        q, k, v = (proj(Wq), proj(Wk), proj(Wv))
        cos, sin = rope_tables(s, HEAD_DIM, x.dtype)
        q = apply_rope_interleaved(q, cos, sin)
        k = apply_rope_interleaved(k, cos, sin)
        scale = 1.0 / jnp.sqrt(jnp.asarray(HEAD_DIM, dtype=x.dtype))
        scores = jnp.einsum('bhqd,bhkd->bhqk', q, k) * scale
        causal = jnp.tril(jnp.ones((s, s), dtype=bool))
        scores = jnp.where(causal[None, None], scores, jnp.asarray(-jnp.inf, dtype=scores.dtype))
        attn = jax.nn.softmax(scores, axis=-1)
        ctx = jnp.einsum('bhqk,bhkd->bhqd', attn, v)
        ctx = ctx.transpose(0, 2, 1, 3).reshape(b, s, N_HEADS * HEAD_DIM)
        return jnp.einsum('bsd,de->bse', ctx, Wo) + bo

    def _L0_xattn_ref(x, y, Wq, bq, Wkv, bkv, Wo, bo):
        import jax, jax.numpy as jnp
        import numpy as np
        N_HEAD = 16
        D_EMBED = 256
        D_CROSS = 192
        D_HEAD = D_EMBED // N_HEAD
        B, SQ, _ = x.shape
        q = x @ Wq + bq
        kv = y @ Wkv + bkv
        k, v = jnp.split(kv, 2, axis=-1)
        q = q.reshape(B, SQ, N_HEAD, D_HEAD).transpose(0, 2, 1, 3)
        k = k.reshape(B, -1, N_HEAD, D_HEAD).transpose(0, 2, 1, 3)
        v = v.reshape(B, -1, N_HEAD, D_HEAD).transpose(0, 2, 1, 3)
        scale = 1.0 / np.sqrt(D_HEAD)
        attn = jnp.einsum('bhqd,bhkd->bhqk', q, k) * scale
        attn = jax.nn.softmax(attn, axis=-1)
        out = jnp.einsum('bhqk,bhkd->bhqd', attn, v)
        out = out.transpose(0, 2, 1, 3).reshape(B, SQ, D_EMBED)
        return out @ Wo + bo

    def _L0_ffn_ref(inputs, gate_weight, ln_gamma, ln_beta, wi, wo, conf_w1, conf_b1, conf_w2, conf_b2, comp_w, comp_b):
        import jax, jax.numpy as jnp
        import numpy as np
        B, L, H, E, I = (4, 512, 256, 8, 1024)
        S = B * L
        CAP_FACTOR_EVAL = 2.0
        MIN_CAP = 4
        _cap = int(np.floor(CAP_FACTOR_EVAL * S / E))
        _cap += _cap % 2
        CAPACITY = max(_cap, MIN_CAP)

        def _layer_norm(x, g, b, eps=1e-05):
            mu = x.mean(-1, keepdims=True)
            var = ((x - mu) ** 2).mean(-1, keepdims=True)
            return (x - mu) * jax.lax.rsqrt(var + eps) * g + b
        tokens = inputs.reshape(-1, H)
        residual = tokens
        tokens = _layer_norm(tokens, ln_gamma, ln_beta)
        complexity_score = jax.nn.sigmoid(tokens @ comp_w.T + comp_b).mean()
        hdn = jax.nn.relu(tokens @ conf_w1.T + conf_b1)
        confidence_score = jax.nn.sigmoid(hdn @ conf_w2.T + conf_b2).mean()
        logits = tokens.astype(jnp.float32) @ gate_weight.astype(jnp.float32).T
        probs = jax.nn.softmax(logits, axis=-1)
        top1 = jnp.argmax(logits, axis=-1)
        onehot = jax.nn.one_hot(top1, E, dtype=jnp.int32)
        rank_e = jnp.cumsum(onehot, axis=0) - onehot
        rank = jnp.sum(rank_e * onehot, axis=-1)
        keep = rank < CAPACITY
        weight = jnp.take_along_axis(probs, top1[:, None], axis=-1)[:, 0]
        weight = (weight * keep).astype(tokens.dtype)
        slot = jnp.where(keep, rank, 0)
        dispatch = jnp.zeros((E, CAPACITY, H), tokens.dtype)
        dispatch = dispatch.at[top1, slot].add(tokens * keep[:, None])
        h = jax.nn.gelu(jnp.einsum('ech,ehi->eci', dispatch, wi), approximate=False)
        expert_out = jnp.einsum('eci,eih->ech', h, wo)
        combined = weight[:, None] * expert_out[top1, slot]
        out = (residual + combined).reshape(inputs.shape)
        return out
    x = x + _L0_attn_ref(_layernorm(x, axis=-1), L0_attn_Wq, L0_attn_Wk, L0_attn_Wv, L0_attn_Wo, L0_attn_bo)
    x = x + _L0_xattn_ref(_layernorm(x, axis=-1), ctx_768, L0_xattn_Wq, L0_xattn_bq, L0_xattn_Wkv, L0_xattn_bkv, L0_xattn_Wo, L0_xattn_bo)
    x = x + _L0_ffn_ref(_layernorm(x, axis=-1), L0_ffn_gate_weight, L0_ffn_ln_gamma, L0_ffn_ln_beta, L0_ffn_wi, L0_ffn_wo, L0_ffn_conf_w1, L0_ffn_conf_b1, L0_ffn_conf_w2, L0_ffn_conf_b2, L0_ffn_comp_w, L0_ffn_comp_b)
    return x

_drawn_inputs = setup_inputs


def setup_inputs(seed=0):
    import zlib

    import numpy as np

    out = dict(_drawn_inputs(seed))
    spreads = {'L0_attn_bo': (0.0, 0.1),
     'L0_xattn_bq': (0.0, 0.382),
     'L0_xattn_bkv': (0.0, 0.1),
     'L0_xattn_bo': (0.0, 0.1),
     'L0_ffn_ln_gamma': (1.0, 0.2),
     'L0_ffn_ln_beta': (0.0, 0.42),
     'L0_ffn_conf_b1': (-1.0, 0.2)}
    factors = {}
    for name, (base, spread) in spreads.items():
        noise = np.random.default_rng([zlib.crc32(name.encode()), seed]).standard_normal(out[name].shape)
        drawn = base * np.exp(spread * noise) if base else spread * noise
        out[name] = jnp.asarray(drawn.astype(out[name].dtype))
    for name, factor in factors.items():
        out[name] = (out[name] * factor).astype(out[name].dtype)
    return out
```

```python
from contextlib import ExitStack

import concourse.bass as bass
from concourse import mybir

P = 128
F32 = mybir.dt.float32
BF16 = mybir.dt.bfloat16
I32 = mybir.dt.int32
ALU = mybir.AluOpType
ACT = mybir.ActivationFunctionType
AX_X = mybir.AxisListType.X

B, S, D = 4, 512, 256
DC = 192
H, HD = 16, 16
E, I, CAP = 8, 1024, 512
N_TOK = B * S
T = S // P
C = D // P
CK = DC // 2
G, GH = 4, 4
IC = I // P
EPS = 1e-5
SCALE = HD ** -0.5
SLOTS = E * CAP

Q_PARTS = (0, 0, 0, 1, 1, 2)
K_PARTS = (0, 1, 2, 0, 1, 0)
SROWS = HD * len(Q_PARTS)
XROWS = SROWS + 2

C_ID, C_PRE, C_MQ, C_MK, C_REV, C_JUNK, C_COS, C_SIN = 0, 128, 256, 384, 512, 520, 524, 588
C_ALL = C_SIN + T * HD


class Ring:

    def __init__(self, uses):
        self.at = {name: n for n, name in enumerate(uses)}
        assert len(self.at) == len(uses) and len(uses) % 2 == 0
        self.n = len(uses)

    def bank(self, name):
        return self.at[name] % 2


def group_uses():
    out = []
    for i in range(G + 3):
        out.append([])
        if i >= 3:
            out[-1].append(("pv", i - 3))
        if 1 <= i <= G:
            out[-1].append(("max", i - 1))
    return out


def batch_uses():
    uses = [("xT", 0), ("xT", 1), ("qk", 0), ("qk", 1), ("v", 0), ("qk", 2), ("qk", 3), ("v", 1)]
    uses += [("rT", j) for j in range(4)]
    for i, step in enumerate(group_uses()):
        uses += [("self",) + u for u in step]
        if i == G + 1:
            uses += [("kc", 0), ("kc", 1)]
    uses += [("vc", 0), ("vc", 1), ("o", 0), ("o", 1)]
    uses += [("yT", 0), ("yT", 1), ("qc", 0), ("qc", 1)]
    for step in group_uses():
        uses += [("cross",) + u for u in step]
    uses += [("xo", 0), ("xo", 1), ("tT", 0), ("tT", 1), ("logit",), ("rank",)]
    return uses


def build(nc, x, ctxT, consts, wqkv, wo, xwq, xwkv, xwo, bq, bk, bv, gamma, beta, gateT, wi, wo_e, out):
    ring = Ring(batch_uses())
    NR = ring.n // 2

    CAUSAL = [[(3,)], [(0,), (2,)], [(1,)]]
    s_uses = {"self": [(h, [q[0] for q in tiles]) for h in range(GH) for tiles in CAUSAL],
              "cross": [(h, [q]) for h in range(GH) for q in range(T)]}
    NS_SELF, NS_CROSS = G * len(s_uses["self"]), G * len(s_uses["cross"])
    NS = NS_SELF + NS_CROSS
    NE_ATT = G * T * 2
    NE = 2 * NE_ATT
    ATT = ("self", "cross")

    spill = nc.dram_tensor("spill", [2, 3, P, S], BF16, kind="Internal")
    disp = nc.dram_tensor("disp", [SLOTS + N_TOK, D], F32, kind="Internal")
    ydram = nc.dram_tensor("ydram", [SLOTS, D], F32, kind="Internal")
    resid = nc.dram_tensor("resid", [B, S, D], F32, kind="Internal")

    with ExitStack() as stack:
        def sb(name, shape, dt=F32):
            return stack.enter_context(nc.sbuf_tensor(name, shape, dt))

        def sem(name):
            return stack.enter_context(nc.semaphore(name))

        cst = sb("cst", [P, C_ALL])
        cosT = cst[:, C_COS:C_COS + T * HD].rearrange("p (t d) -> p t d", t=T)
        sinT = cst[:, C_SIN:C_SIN + T * HD].rearrange("p (t d) -> p t d", t=T)
        identf = cst[:, C_ID:C_ID + P]
        cstb = sb("cstb", [P, 4 * P], BF16)
        identb, prefb, maskqb, maskkb = (cstb[:, n * P:(n + 1) * P] for n in range(4))
        onesb = sb("onesb", [P, P], BF16)
        wqkv_sb = sb("wqkv_sb", [P, C, 3 * D])
        wo_sb = sb("wo_sb", [P, G, D])
        xwq_sb = sb("xwq_sb", [P, C, D])
        xwkv_sb = sb("xwkv_sb", [CK, 2, 2 * D])
        xwo_sb = sb("xwo_sb", [P, G, D])
        bq_sb = sb("bq_sb", [P, C])
        bk_sb = sb("bk_sb", [P, C])
        bv_sb = sb("bv_sb", [P, D])
        gam_sb = sb("gam_sb", [P, D])
        bet_sb = sb("bet_sb", [P, D])
        gate_sb = sb("gate_sb", [P, C, E])

        xb = sb("xb", [P, T, D])
        x1 = sb("x1", [P, T, D])
        xn = sb("xn", [P, T, D])
        tok = sb("tok", [P, T, D])
        xnT = sb("xnT", [P, C, S])
        ctx_sb = sb("ctx_sb", [CK, 2, S])
        rc = sb("rc", [P, 2, 2 * D])
        rs = sb("rs", [P, 2, 2 * D])
        att = sb("att", [P, G, S])
        rot = att
        src32 = sb("src32", [P, 2, S])
        rem32 = sb("rem32", [P, 2, S])
        parts = sb("parts", [P, 2, 3, S], BF16)
        V = {a: sb("v_" + a, [P, T, H, 2 * HD]) for a in ATT}
        rowsum = sb("rowsum", [P, 2, S])
        mx = sb("mx", [P, 2, GH, T])
        nmx = sb("nmx", [P, 2, 2, GH * T], BF16)
        mrow = sb("mrow", [2 * GH * T, 2, P], BF16)
        stats = sb("stats", [P, T, 6])
        mv = sb("mv", [P, T, 2])
        rstd = sb("rstd", [P, T])
        rsq = sb("rsq", [P, T])
        newton = sb("newton", [P, 2, T])
        var2 = sb("var2", [P, T])
        rstd2 = sb("rstd2", [P, T])
        z = sb("z", [P, T, E])
        ez = sb("ez", [P, T, E])
        cand = sb("cand", [P, T, E])
        onehot = sb("onehot", [P, T, E])
        onehotb = sb("onehotb", [P, T, E], BF16)
        rk = sb("rk", [P, T, E])
        count = sb("count", [P, E])
        small = sb("small", [P, 12, T])
        junk = sb("junk", [P, T])
        sidx = sb("sidx", [P, T], I32)
        gidx = sb("gidx", [P, B, T], I32)
        wtok = sb("wtok", [P, B, T])
        wi_sb = sb("wi_sb", [P, 2, C, I])
        slab = sb("slab", [P, 8192 + 3 * 4096])
        prob = slab[:, 0:8192].rearrange("p (t h s) -> p t h s", t=T, h=GH)
        stk = {name: slab[:, 8192 + n * 4096:8192 + (n + 1) * 4096].bitcast(BF16).rearrange("p (h s) -> p h s", h=H)
               for n, name in enumerate(("q", "self", "cross"))}
        o = 0

        def carve(n):
            nonlocal o
            o += n
            return slab[:, o - n:o]
        woe_sb = carve(2 * IC * D).rearrange("p (b c d) -> p b c d", b=2, c=IC)
        hT = carve(IC * CAP).rearrange("p (c s) -> p c s", c=IC)
        dsp = carve(2 * T * D).rearrange("p (b t d) -> p b t d", b=2, t=T)
        dspT = carve(2 * C * CAP).rearrange("p (b c s) -> p b c s", b=2, c=C)
        yb = carve(2 * T * D).rearrange("p (b t d) -> p b t d", b=2, t=T)
        yg = hT.rearrange("p c s -> p (c s)").rearrange("p (n d) -> p n d", n=16)
        rg = slab[:, o - 16 * D:o].rearrange("p (n d) -> p n d", n=16)

        ps = stack.enter_context(nc.psum_tensor("ps", [P, 8, S], F32))
        s_bank = [ps[:, n, :] for n in (0, 1)]
        e_bank = [ps[:, 2:4, :], ps[:, 4:6, :]]
        r_bank = [ps[:, n, :] for n in (6, 7)]

        d_cst, d_w, d_x, d_ctx, d_out, d_zero, d_wi0 = (sem(n) for n in ("d_cst", "d_w", "d_x", "d_ctx", "d_out", "d_zero", "d_wi0"))
        c_ready, v_ready, z_ready = sem("c_ready"), sem("v_ready"), sem("z_ready")
        ring_full = [sem("ring_full0"), sem("ring_full1")]
        ring_moved = [sem("ring_moved0"), sem("ring_moved1")]
        xn_ready = sem("xn_ready")
        rot_ready = sem("rot_ready")
        hi_ready = sem("hi_ready")
        rem_ready = sem("rem_ready")
        mid_ready = sem("mid_ready")
        lo_ready = sem("lo_ready")
        d_spill = [sem("d_spill0"), sem("d_spill1")]
        d_stack = [sem(f"d_stack{n}") for n in range(8)]
        s_full, s_free = sem("s_full"), sem("s_free")
        mx_ready = sem("mx_ready")
        d_max = [sem(f"d_max{g}") for g in range(G)]
        e_full, e_done = sem("e_full"), sem("e_done")
        sum_ready = sem("sum_ready")
        res_ready, d_res = sem("res_ready"), sem("d_res")
        tokg_ready = sem("tokg_ready")
        tok_ready = sem("tok_ready")
        ez_ready, oh_ready = sem("ez_ready"), sem("oh_ready")
        idx_ready, d_scat = sem("idx_ready"), sem("d_scat")
        chain = sem("chain")
        t_full, t_free, h_full, h_free, y_full, y_free = (sem(n) for n in ("t_full", "t_free", "h_full", "h_free", "y_full", "y_free"))
        d_wi = [sem("d_wi0_"), sem("d_wi1_")]
        d_wo = [sem("d_wo0_"), sem("d_wo1_")]
        d_dsp = [sem("d_dsp0"), sem("d_dsp1")]
        d_y = [sem("d_y0"), sem("d_y1")]
        d_rg, d_yg = sem("d_rg"), [sem(f"d_yg{n}") for n in range(16)]
        o_ready = sem("o_ready")

        held, held_pool = sem("held"), sem("held_pool")
        N_CHAIN = 78

        block = stack.enter_context(nc.Block())

        SPLITS = [("rT", n) for n in range(4)] + [("kc", 0), ("kc", 1), ("qc", 0), ("qc", 1)]

        def full(eng, b, name):
            eng.wait_ge(ring_full[ring.bank(name)], b * NR + ring.at[name] // 2 + 1)

        def bank(name):
            return r_bank[ring.bank(name)]

        def filled(ins, name):
            ins.then_inc(ring_full[ring.bank(name)], 1)

        def moved(eng, b, *names):
            for n in (0, 1):
                counts = [ring.at[name] // 2 + 1 for name in names if ring.bank(name) == n]
                if counts:
                    eng.wait_ge(ring_moved[n], b * NR + max(counts))

        def moves(ins, name):
            ins.then_inc(ring_moved[ring.bank(name)], 1)

        @block.sync
        def _(sp):
            def stack_job(b, n, kind, c):
                par, parts_of = n % 2, (Q_PARTS if kind == "q" else K_PARTS)
                sp.wait_ge(lo_ready, b * 8 + n + 1)
                sp.dma_start(spill[par].rearrange("j p n -> p j n"), parts[:, par, :, :]).then_inc(d_spill[par], 16)
                sp.wait_ge(d_spill[par], b * 64 + 16 * (n // 2 + 1))
                for i, j in enumerate(parts_of):
                    sp.dma_start(stk["q" if kind == "q" else kind][16 * i:16 * i + 16, 8 * c:8 * c + 8, :],
                                 spill[par, j].rearrange("(h d) n -> d h n", h=8)).then_inc(d_stack[n], 16)

            def max_job(b, a, g):
                k = a * G + g
                moved(sp, b, (ATT[a], "max", g))
                for part in range(2):
                    sp.dma_start(stk["q"][SROWS + part:SROWS + part + 1, GH * g:GH * g + GH, :].rearrange("p h (t c) -> p (h t) c", c=P),
                                 mrow[16 * part:16 * part + 16, k % 2, :]).then_inc(d_max[g], 16)

            sp.dma_start(cst[:, :], consts).then_inc(d_cst, 16)
            sp.dma_start(xb[:, :, :], x[0].rearrange("(t p) d -> p t d", p=P)).then_inc(d_x, 16)
            sp.dma_start(wqkv_sb[:, :, :], wqkv.rearrange("(c p) n -> p c n", p=P)).then_inc(d_w, 16)
            for dst, src in ((wo_sb, wo), (xwq_sb, xwq), (xwo_sb, xwo), (gate_sb, gateT)):
                sp.dma_start(dst[:, :, :], src.rearrange("(c p) n -> p c n", p=P)).then_inc(d_w, 16)
            sp.dma_start(xwkv_sb[:, :, :], xwkv.rearrange("(c p) n -> p c n", p=CK)).then_inc(d_w, 16)
            for dst, src in ((bq_sb, bq), (bk_sb, bk), (bv_sb, bv), (gam_sb, gamma), (bet_sb, beta)):
                sp.dma_start(dst[:, :], src).then_inc(d_w, 16)
            sp.wait_ge(z_ready, 1)
            for n in range(E):
                sp.dma_start(disp[n * CAP:(n + 1) * CAP, :].rearrange("(t p) d -> p t d", p=P),
                             slab[:, 0:T * D].rearrange("p (t d) -> p t d", t=T)).then_inc(d_zero, 16)
            with sp.Fori(0, B) as b:
                for use_done in ring_full:
                    sp.wait_ge(use_done, b * NR)
                sp.dma_start(ctx_sb[:, :, :], ctxT[b].rearrange("(c p) n -> p c n", p=CK)).then_inc(d_ctx, 16)
                for n, (kind, c) in enumerate((("q", 0), ("self", 0), ("q", 1), ("self", 1))):
                    stack_job(b, n, kind, c)
                for g in range(G):
                    max_job(b, 0, g)
                for n in (4, 5):
                    stack_job(b, n, "cross", n - 4)
                for n in (6, 7):
                    stack_job(b, n, "q", n - 6)
                moved(sp, b, ("o", 1))
                sp.dma_start(xb[:, :, :], x[(b + 1) % B].rearrange("(t p) d -> p t d", p=P)).then_inc(d_x, 16)
                for g in range(G):
                    max_job(b, 1, g)
                sp.wait_ge(res_ready, b + 1)
                sp.dma_start(resid[b].rearrange("(t p) d -> p t d", p=P), xn[:, :, :]).then_inc(d_res, 16)

            sp.wait_ge(d_scat, B * T * 16)

            def load_w(e, par):
                sp.dma_start(wi_sb[:, par, :, :], wi[e].rearrange("(c p) n -> p c n", p=P)).then_inc(d_wi[par], 16)
                sp.dma_start(woe_sb[:, par, :, :], wo_e[e].rearrange("(c p) n -> p c n", p=P)).then_inc(d_wo[par], 16)
                sp.dma_start(dsp[:, par, :, :], disp[bass.ds(e * CAP, CAP), :].rearrange("(t p) d -> p t d", p=P)).then_inc(d_dsp[par], 16)

            for use_done in ring_full:
                sp.wait_ge(use_done, B * NR)
            for par in range(2):
                load_w(par, par)
            with sp.Fori(0, E // 2) as u:
                for par in range(2):
                    sp.wait_ge(y_free, u * 4 + 2 * par + 2)
                    sp.dma_start(ydram[bass.ds(u * (2 * CAP) + par * CAP, CAP), :].rearrange("(t p) d -> p t d", p=P),
                                 yb[:, par, :, :]).then_inc(d_y[par], 16)
                    load_w((u * 2 + (par + 2)) % E, par)
            for par in range(2):
                sp.wait_ge(d_y[par], 8 * E)
            for b in range(B):
                sp.dma_start(rg[:, 4 * b:4 * b + 4, :], resid[b].rearrange("(t p) d -> p t d", p=P)).then_inc(d_rg, 16)
            for b in range(B):
                sp.wait_ge(o_ready, 4 * b + 4)
                sp.dma_start(out[b].rearrange("(t p) d -> p t d", p=P), rg[:, 4 * b:4 * b + 4, :]).then_inc(d_out, 16)
            sp.wait_ge(d_out, 16 * B)
            sp.wait_ge(d_x, 16 * (B + 1))
            for par in range(2):
                for d in (d_wi, d_wo, d_dsp):
                    sp.wait_ge(d[par], 8 * E + 16)

        @block.gpsimd
        def _(pool):
            pool.memset(slab[:, 0:T * D], 0.0).then_inc(z_ready, 1)
            pool.memset(onesb[:, :], 1.0).then_inc(c_ready, 1)
            pool.memset(count[:, :], 0.0).then_inc(c_ready, 1)
            for a in ATT:
                pool.memset(V[a][:, :, :, HD:2 * HD], 1.0).then_inc(v_ready, 1)
            pool.wait_ge(v_ready, 2)
            pool.memset(stk["self"][SROWS:XROWS, :, :], 1.0).then_inc(v_ready, 1)
            pool.wait_ge(v_ready, 3)
            pool.memset(stk["cross"][SROWS:XROWS, :, :], 1.0).then_inc(v_ready, 1)
            pool.wait_ge(v_ready, 4)

            def split(b, n):
                par = n % 2
                pool.wait_ge(hi_ready, b * 8 + n + 1)
                pool.tensor_tensor(rem32[:, par, :], src32[:, par, :], parts[:, par, 0, :], ALU.subtract).then_inc(rem_ready, 1)
                pool.wait_ge(mid_ready, b * 8 + n + 1)
                pool.tensor_tensor(parts[:, par, 2, :], rem32[:, par, :], parts[:, par, 1, :], ALU.subtract).then_inc(lo_ready, 1)

            pool.wait_ge(d_w, 16 * 11)
            with pool.Fori(0, B) as b:
                for t in range(T):
                    moved(pool, b, ("qk", t))
                    pool.tensor_tensor(rot[:, t, :], rc[:, t % 2, :], rs[:, t % 2, :], ALU.add).then_inc(rot_ready, 1)
                for n in range(8):
                    split(b, n)
                for t in range(T):
                    pool.wait_ge(tokg_ready, b * T + t + 1)
                    pool.tensor_tensor(tok[:, t, :], tok[:, t, :], bet_sb[:, :], ALU.add).then_inc(tok_ready, 1)
                moved(pool, b, ("xo", 1))
                pool.tensor_tensor(xn[:, :, :], xn[:, :, :], x1[:, :, :], ALU.add).then_inc(res_ready, 1)
                pool.wait_ge(idx_ready, b + 1)
                pool.sem_inc(held_pool, 1)
                pool.wait_ge(d_zero, 16 * E)
                for t in range(T):
                    pool.indirect_dma_start(disp[:, :], bass.IndirectOffsetOnAxis(ap=sidx[:, t:t + 1], axis=0),
                                            tok[:, t, :], None).then_inc(d_scat, 16)
                pool.wait_ge(d_scat, b * (16 * T) + 16 * T)
            for par in range(2):
                pool.wait_ge(d_y[par], 8 * E)
            for n in range(16):
                pool.indirect_dma_start(yg[:, n, :], None, ydram[:, :],
                                        bass.IndirectOffsetOnAxis(ap=gidx[:, n // T, n % T:n % T + 1], axis=0)).then_inc(d_yg[n], 16)

        @block.scalar
        def _(act):
            def exps(b, a, g):
                if g == 0:
                    act.wait_ge(d_zero, 16 * E)
                for kt in range(T):
                    q0 = kt * P if a == 0 else 0
                    for pair in range(2):
                        n = a * NE_ATT + (g * T + kt) * 2 + pair
                        act.wait_ge(e_full, b * NE + n + 1)
                        act.activation(prob[:, kt, 2 * pair:2 * pair + 2, q0:S], e_bank[n % 2][:, :, q0:S], ACT.Exp,
                                       scale=SCALE).then_inc(e_done, 1)

            act.wait_ge(d_w, 16 * 11)
            with act.Fori(0, B) as b:
                def move(name, dst, func, src=None, **kw):
                    full(act, b, name)
                    moves(act.activation(dst, bank(name) if src is None else src, func, **kw), name)

                def to_split(name, n, **kw):
                    act.wait_ge(rem_ready, b * 8 + (n - 1 if n >= 2 else 0))
                    move(name, src32[:, n % 2, :], ACT.Identity if kw else ACT.Copy, **kw)

                for c in range(C):
                    move(("xT", c), xnT[:, c, :], ACT.Copy)
                for n in range(2):
                    move(("v", n), V["self"][:, 2 * n:2 * n + 2, :, 0:HD], ACT.Copy,
                         src=bank(("v", n)).rearrange("p (t h d) -> p t h d", t=2, h=H))
                for n in range(4):
                    to_split(("rT", n), n)
                for g in range(G):
                    exps(b, 0, g)
                for m in range(C):
                    to_split(("kc", m), 4 + m, bias=bk_sb[:, m:m + 1])
                for c in range(C):
                    move(("yT", c), xnT[:, c, :], ACT.Copy)
                for m in range(C):
                    to_split(("qc", m), 6 + m, bias=bq_sb[:, m:m + 1])
                for g in range(G):
                    exps(b, 1, g)
                for c in range(C):
                    move(("tT", c), xnT[:, c, :], ACT.Copy)
                moved(act, b, ("logit",))
                act.activation(ez[:, :, :], z[:, :, :], ACT.Exp).then_inc(ez_ready, 1)
            with act.Fori(0, E // 2) as u:
                for par in range(2):
                    for c in range(C):
                        act.wait_ge(t_full, u * 4 + par * 2 + c + 1)
                        act.activation(dspT[:, par, c, :], s_bank[c], ACT.Copy).then_inc(t_free, 1)
                    for n in range(IC):
                        act.wait_ge(h_full, u * (2 * IC) + par * IC + n + 1)
                        act.activation(hT[:, n, :], ps[:, 2 + n % 4, :], ACT.Gelu).then_inc(h_free, 1)

        @block.tensor
        def _(pe):
            def take(b, name, *reads):
                for n in (0, 1):
                    counts = [ring.at[r] // 2 + 1 for r in reads if ring.bank(r) == n]
                    counts += [ring.at[name] // 2] * (ring.bank(name) == n)
                    if counts:
                        pe.wait_ge(ring_moved[n], b * NR + max(counts))
                return bank(name)

            def turn(b, name, src, ready, base):
                dst = take(b, name)
                for t in range(T):
                    pe.wait_ge(ready, base + t + 1)
                    mm = pe.transpose(dst[:, t * P:(t + 1) * P], src(t), identf)
                filled(mm, name)

            def score(b, a, g, n):
                name = ATT[a]
                hh, tiles = s_uses[name][n]
                h = GH * g + hh
                k = a * NS_SELF + g * len(s_uses[name]) + n
                pe.wait_ge(s_free, b * NS + (k - 1 if k else 0))
                o = 0
                for qt in tiles:
                    w = (qt + 1) * P if a == 0 else S
                    dst = s_bank[k % 2]
                    mm = pe.matmul(dst[:, o:o + w], stk["q"][0:SROWS, h, qt * P:(qt + 1) * P], stk[name][0:SROWS, h, 0:w],
                                   start=True, stop=True)
                    if a == 0:
                        mm = pe.matmul(dst[:, o + w - P:o + w], identb, maskqb, start=False, stop=True, skip_group_check=True)
                    o += w
                mm.then_inc(s_full, 1)

            def score_T(b, a, g, kt, pair):
                name = ATT[a]
                n = a * NE_ATT + (g * T + kt) * 2 + pair
                pe.wait_ge(e_done, b * NE + (n - 1 if n else 0))
                q0 = kt * P if a == 0 else 0
                for i in range(2):
                    h = GH * g + 2 * pair + i
                    dst = e_bank[n % 2][:, i, :]
                    mm = pe.matmul(dst[:, q0:S], stk[name][0:XROWS, h, kt * P:(kt + 1) * P], stk["q"][0:XROWS, h, q0:S],
                                   start=True, stop=True)
                    if a == 0:
                        mm = pe.matmul(dst[:, q0:q0 + P], identb, maskkb, start=False, stop=True, skip_group_check=True)
                mm.then_inc(e_full, 1)

            def values(b, a, g, kt):
                name = (ATT[a], "pv", g)
                dst = take(b, name) if kt == 0 else bank(name)
                pe.wait_ge(e_done, b * NE + a * NE_ATT + (g * T + kt) * 2 + 2)
                q0 = kt * P if a == 0 else 0
                for i in range(GH):
                    mm = pe.matmul(dst[32 * i:32 * i + 32, q0:S], V[ATT[a]][:, kt, GH * g + i, :], prob[:, kt, i, q0:S],
                                   start=(kt == 0), stop=True, skip_group_check=True)
                if kt == T - 1:
                    filled(mm, name)

            def turn_max(b, a, g):
                dst = take(b, (ATT[a], "max", g)).bitcast(BF16)
                pe.wait_ge(mx_ready, b * 2 * G + a * G + g + 1)
                filled(pe.transpose(dst[0:2 * GH * T, 0:P], nmx[:, (a * G + g) % 2, :, :].rearrange("p j n -> p (j n)"), identb),
                       (ATT[a], "max", g))

            def attend(b, a):
                name = ATT[a]
                q_sem, k_sem = ((d_stack[0], d_stack[2]), (d_stack[1], d_stack[3])) if a == 0 else \
                               ((d_stack[6], d_stack[7]), (d_stack[4], d_stack[5]))
                for i in range(G + 3):
                    for q in range(T):
                        if i >= 3:
                            values(b, a, i - 3, q)
                        for j in range(4):
                            n = 4 * q + j
                            if i < G and n < len(s_uses[name]):
                                if n == 0 and i % 2 == 0:
                                    pe.wait_ge(q_sem[i // 2], b * 96 + 96)
                                    pe.wait_ge(k_sem[i // 2], b * 96 + 96)
                                score(b, a, i, n)
                            if 2 <= i < G + 2 and j % 2 == 0:
                                if q == 0 and j == 0:
                                    pe.wait_ge(d_max[i - 2], b * 64 + a * 32 + 32)
                                score_T(b, a, i - 2, q, j // 2)
                        if q == 0 and 1 <= i <= G:
                            turn_max(b, a, i - 1)
                    if a == 0 and i == G + 1:
                        pe.wait_ge(d_ctx, b * 16 + 16)
                        for m in range(C):
                            dst = take(b, ("kc", m))
                            for c in range(2):
                                mm = pe.matmul(dst, xwkv_sb[:, c, m * P:(m + 1) * P], ctx_sb[:, c, :], start=(c == 0), stop=(c == 1))
                            filled(mm, ("kc", m))

            def project(b, name, w, a):
                for n in range(2):
                    dst = take(b, (name, n), *((ATT[a], "pv", g) for g in range(G)))
                    for i in range(2):
                        for g in range(G):
                            mm = pe.matmul(dst[:, i * D:(i + 1) * D], att[:, g, (2 * n + i) * P:(2 * n + i + 1) * P], w[:, g, :],
                                           start=(g == 0), stop=(g == G - 1))
                    filled(mm, (name, n))

            pe.wait_ge(d_cst, 16)
            pe.wait_ge(c_ready, 4)
            pe.wait_ge(v_ready, 4)
            pe.wait_ge(d_w, 16 * 11)
            with pe.Fori(0, B) as b:
                for c in range(C):
                    turn(b, ("xT", c), lambda t: xn[:, t, c * P:(c + 1) * P], xn_ready, b * 3 * T)
                for half in range(2):
                    for t in (2 * half, 2 * half + 1):
                        dst = take(b, ("qk", t), ("xT", 0), ("xT", 1))
                        for c in range(C):
                            mm = pe.matmul(dst, xnT[:, c, t * P:(t + 1) * P], wqkv_sb[:, c, 0:2 * D], start=(c == 0), stop=(c == C - 1))
                        filled(mm, ("qk", t))
                    dst = take(b, ("v", half))
                    for i in range(2):
                        t = 2 * half + i
                        for c in range(C):
                            mm = pe.matmul(dst[:, i * D:(i + 1) * D], xnT[:, c, t * P:(t + 1) * P], wqkv_sb[:, c, 2 * D:3 * D],
                                           start=(c == 0), stop=(c == C - 1))
                    filled(mm, ("v", half))
                for n, j in enumerate((0, 2, 1, 3)):
                    turn(b, ("rT", n), lambda t: rot[:, t, j * P:(j + 1) * P], rot_ready, b * T)
                moved(pe, b, ("v", 0), ("v", 1))
                attend(b, 0)
                for half in range(2):
                    dst = take(b, ("vc", half))
                    for i in range(2):
                        t = 2 * half + i
                        for c in range(2):
                            mm = pe.matmul(dst[:, i * D:(i + 1) * D], ctx_sb[:, c, t * P:(t + 1) * P], xwkv_sb[:, c, D:2 * D],
                                           start=(c == 0), stop=(c == 1))
                    filled(mm, ("vc", half))
                project(b, "o", wo_sb, 0)
                for c in range(C):
                    turn(b, ("yT", c), lambda t: xn[:, t, c * P:(c + 1) * P], xn_ready, b * 3 * T + T)
                for m in range(C):
                    dst = take(b, ("qc", m), ("yT", 0), ("yT", 1))
                    for c in range(C):
                        mm = pe.matmul(dst, xwq_sb[:, c, m * P:(m + 1) * P], xnT[:, c, :], start=(c == 0), stop=(c == C - 1))
                    filled(mm, ("qc", m))
                moved(pe, b, ("vc", 0), ("vc", 1))
                attend(b, 1)
                project(b, "xo", xwo_sb, 1)
                for c in range(C):
                    turn(b, ("tT", c), lambda t: tok[:, t, c * P:(c + 1) * P], tok_ready, b * T)
                dst = take(b, ("logit",), ("tT", 0), ("tT", 1))
                for t in range(T):
                    for c in range(C):
                        mm = pe.matmul(dst[:, t * E:(t + 1) * E], xnT[:, c, t * P:(t + 1) * P], gate_sb[:, c, :],
                                       start=(c == 0), stop=(c == C - 1))
                filled(mm, ("logit",))
                dst = take(b, ("rank",))
                pe.wait_ge(oh_ready, b + 1)
                oh = onehotb[:, :, :].rearrange("p t e -> p (t e)")
                pe.matmul(dst[:, 0:T * E], prefb, oh, start=True, stop=True, skip_group_check=True)
                for k in range(1, T):
                    pe.matmul(dst[:, k * E:T * E], onesb[:, :], oh[:, 0:(T - k) * E], start=False, stop=True, skip_group_check=True)
                for t in range(T):
                    mm = pe.matmul(dst[:, T * E:(T + 1) * E], onesb[:, :], oh[:, t * E:(t + 1) * E], start=False,
                                   stop=True, skip_group_check=True)
                filled(mm, ("rank",))

            def turn_slots(par, loads, used):
                pe.wait_ge(d_dsp[par], loads)
                for c in range(C):
                    if used is not None:
                        pe.wait_ge(t_free, used + c)
                    for t in range(T):
                        mm = pe.transpose(s_bank[c][:, t * P:(t + 1) * P], dsp[:, par, t, c * P:(c + 1) * P], identf)
                    mm.then_inc(t_full, 1)

            pe.wait_ge(s_free, B * NS)
            turn_slots(0, 16, None)
            pe.wait_ge(e_done, B * NE)
            for bank_moved in ring_moved:
                pe.wait_ge(bank_moved, B * NR)
            with pe.Fori(0, E // 2) as u:
                for par in range(2):
                    pe.wait_ge(t_free, u * 4 + 2 * par + 2)
                    pe.wait_ge(d_wi[par], u * 16 + 16)
                    for n in range(IC):
                        k = par * IC + n
                        pe.wait_ge(h_free, u * (2 * IC) + max(k - 3, 0))
                        for c in range(C):
                            mm = pe.matmul(ps[:, 2 + n % 4, :], wi_sb[:, par, c, n * P:(n + 1) * P], dspT[:, par, c, :],
                                           start=(c == 0), stop=(c == C - 1))
                        mm.then_inc(h_full, 1)
                    turn_slots(1 - par, (u + par) * 16 + 16, u * 4 + 2 * par + 1)
                    pe.wait_ge(d_wo[par], u * 16 + 16)
                    pe.wait_ge(h_free, u * (2 * IC) + (par + 1) * IC)
                    for half in range(2):
                        k = 2 * par + half
                        pe.wait_ge(y_free, u * 4 + max(k - 1, 0))
                        for i in range(2):
                            t = 2 * half + i
                            for n in range(IC):
                                mm = pe.matmul(r_bank[half][:, i * D:(i + 1) * D], hT[:, n, t * P:(t + 1) * P], woe_sb[:, par, n, :],
                                               start=(n == 0), stop=(n == IC - 1))
                        mm.then_inc(y_full, 1)

        @block.vector
        def _(dve):
            links = [0]

            def hold():
                dve.sem_inc(held, 1)

            def link(b, ins, plain=False):
                links[0] += 1
                ins.then_inc(chain, 1)
                dve.wait_ge(chain, b * N_CHAIN + links[0])
                if plain:
                    hold()

            def rsqrt(b, dst, var):
                v, guess = newton[:, 0, :], newton[:, 1, :]
                link(b, dve.tensor_scalar(v, var, EPS, None, ALU.add))
                link(b, dve.tensor_scalar(guess.bitcast(I32), v.bitcast(I32), 1, None, ALU.logical_shift_right))
                link(b, dve.tensor_scalar(dst.bitcast(I32), guess.bitcast(I32), -1.0, float(0x5f3759df), ALU.mult, ALU.add))
                for _ in range(3):
                    link(b, dve.tensor_tensor(guess, dst, dst, ALU.mult))
                    link(b, dve.scalar_tensor_tensor(out=guess, in0=guess, scalar=-0.5, in1=v, op0=ALU.mult, op1=ALU.mult))
                    link(b, dve.scalar_tensor_tensor(out=dst, in0=guess, scalar=1.5, in1=dst, op0=ALU.add, op1=ALU.mult))

            def norm_stats(b, src):
                for t in range(T):
                    i = dve.bn_stats(stats[:, t, :], src[:, t, :])
                link(b, i, plain=True)
                for t in range(T):
                    i = dve.bn_aggr(mv[:, t, :], stats[:, t, :])
                link(b, i)
                rsqrt(b, rstd[:, :], mv[:, :, 1])

            def norm_apply(src):
                for t in range(T):
                    dve.tensor_scalar(xn[:, t, :], src[:, t, :], mv[:, t, 0:1], rstd[:, t:t + 1], ALU.subtract, ALU.mult).then_inc(xn_ready, 1)

            def rope(b, t):
                full(dve, b, ("qk", t))
                if t >= 2:
                    dve.wait_ge(rot_ready, b * T + t - 1)
                src = bank(("qk", t)).rearrange("p (h d) -> p h d", d=HD)
                pr = src.rearrange("p h (i two) -> p h i two", two=2)
                o = rs[:, t % 2, :].rearrange("p (h i two) -> p h i two", h=2 * H, two=2)
                sn = sinT[:, t, :].rearrange("p (i two) -> p i two", two=2)
                dve.tensor_tensor(rc[:, t % 2, :].rearrange("p (h d) -> p h d", d=HD), src,
                                  cosT[:, t:t + 1, :].to_broadcast([P, 2 * H, HD]), ALU.mult)
                for k in range(2):
                    i = dve.tensor_tensor(o[:, :, :, k], pr[:, :, :, 1 - k],
                                          sn[:, :, k:k + 1].rearrange("p i o -> p o i").to_broadcast([P, 2 * H, HD // 2]),
                                          ALU.mult)
                moves(i, ("qk", t))

            def split(b, n):
                par = n % 2
                moved(dve, b, SPLITS[n])
                dve.wait_ge(d_spill[par], b * 64 + 16 * (n // 2))
                dve.tensor_copy(parts[:, par, 0, :], src32[:, par, :]).then_inc(hi_ready, 1)
                dve.wait_ge(rem_ready, b * 8 + n + 1)
                dve.tensor_copy(parts[:, par, 1, :], rem32[:, par, :]).then_inc(mid_ready, 1)

            def maxima(b, a, g, n):
                name = ATT[a]
                hh, tiles = s_uses[name][n]
                k = a * NS_SELF + g * len(s_uses[name]) + n
                dve.wait_ge(s_full, b * NS + k + 1)
                o = 0
                for qt in tiles:
                    w = (qt + 1) * P if a == 0 else S
                    i = dve.tensor_reduce(mx[:, (a * G + g) % 2, hh, qt:qt + 1], s_bank[k % 2][:, o:o + w], AX_X, ALU.max)
                    o += w
                i.then_inc(s_free, 1)

            def negate(b, a, g):
                par = (a * G + g) % 2
                dve.wait_ge(s_free, b * NS + a * NS_SELF + (g + 1) * len(s_uses[ATT[a]]))
                m = mx[:, par, :, :].rearrange("p h t -> p (h t)")
                link(b, dve.tensor_scalar(nmx[:, par, 0, :], m, -1.0, None, ALU.mult))
                dve.scalar_tensor_tensor(out=nmx[:, par, 1, :], in0=m, scalar=-1.0, in1=nmx[:, par, 0, :],
                                         op0=ALU.mult, op1=ALU.subtract).then_inc(mx_ready, 1)

            def max_rows(b, a, g):
                name = (ATT[a], "max", g)
                par = (a * G + g) % 2
                full(dve, b, name)
                if a or g >= 2:
                    k = (a * G + g - 2)
                    dve.wait_ge(d_max[k % G], b * 64 + (k // G) * 32 + 32)
                else:
                    dve.wait_ge(d_max[(g - 2) % G], b * 64)
                moves(dve.tensor_copy(mrow[:, par, :], bank(name).bitcast(BF16)[0:2 * GH * T, 0:P]), name)

            def normalise(b, a, g):
                name = (ATT[a], "pv", g)
                full(dve, b, name)
                hold()
                par = g % 2
                dve.stream_shuffle(rowsum[:, par, :], bank(name), [HD] * 32).then_inc(sum_ready, 1)
                dve.wait_ge(sum_ready, b * 4 * G + 2 * (a * G + g) + 1)
                dve.reciprocal(rowsum[:, par, :], rowsum[:, par, :]).then_inc(sum_ready, 1)
                dve.wait_ge(sum_ready, b * 4 * G + 2 * (a * G + g) + 2)
                moves(dve.tensor_tensor(att[:, g, :], bank(name), rowsum[:, par, :], ALU.mult), name)

            def attend(b, a):
                for i in range(G + 3):
                    for n in range(16):
                        if i < G and n < len(s_uses[ATT[a]]):
                            maxima(b, a, i, n)
                        if n == 5 and 1 <= i <= G:
                            max_rows(b, a, i - 1)
                    if i < G:
                        negate(b, a, i)
                    if i >= 3:
                        normalise(b, a, i - 3)
                    if a == 0 and i == G + 1:
                        split(b, 4)
                        split(b, 5)

            def add_rows(b, name, src):
                for n in range(2):
                    full(dve, b, (name, n))
                    moves(dve.tensor_tensor(x1[:, 2 * n:2 * n + 2, :], bank((name, n)).rearrange("p (t d) -> p t d", t=2),
                                            src[:, 2 * n:2 * n + 2, :], ALU.add), (name, n))
                moved(dve, b, (name, 0), (name, 1))

            def route(b):
                def col(k):
                    return small[:, k, :]

                def wide(k):
                    return small[:, k, :].rearrange("p (t o) -> p t o", o=1).to_broadcast([P, T, E])

                rev = cst[:, C_REV:C_REV + E].rearrange("p (o e) -> p o e", o=1).to_broadcast([P, T, E])
                TOP, LAST, DEN, PROB, RANK, KEEP, BASE, KRANK, DIFF, PICK = range(10)
                full(dve, b, ("logit",))
                logit = bank(("logit",))[:, 0:T * E].rearrange("p (t e) -> p t e", t=T)
                link(b, dve.tensor_reduce(col(TOP), logit, AX_X, ALU.max))
                moves(dve.tensor_tensor(z[:, :, :], logit, wide(TOP), ALU.subtract), ("logit",))
                moved(dve, b, ("logit",))
                link(b, dve.scalar_tensor_tensor(out=cand[:, :, :], in0=z[:, :, :], scalar=0.0, in1=rev, op0=ALU.is_ge, op1=ALU.mult))
                link(b, dve.tensor_reduce(col(LAST), cand[:, :, :], AX_X, ALU.max))
                link(b, dve.tensor_tensor(onehot[:, :, :], rev, wide(LAST), ALU.is_equal))
                dve.tensor_copy(onehotb[:, :, :], onehot[:, :, :]).then_inc(oh_ready, 1)
                dve.wait_ge(ez_ready, b + 1)
                link(b, dve.tensor_reduce(col(DEN), ez[:, :, :], AX_X, ALU.add))
                dve.reciprocal(col(PROB), col(DEN))
                full(dve, b, ("rank",))
                pr = bank(("rank",))
                link(b, dve.tensor_tensor(rk[:, :, :], pr[:, 0:T * E].rearrange("p (t e) -> p t e", t=T),
                                          count[:, :].rearrange("p (o e) -> p o e", o=1).to_broadcast([P, T, E]), ALU.add))
                moves(dve.tensor_tensor(count[:, :], pr[:, T * E:(T + 1) * E], count[:, :], ALU.add), ("rank",))
                link(b, dve.tensor_tensor(rk[:, :, :], rk[:, :, :], onehot[:, :, :], ALU.mult))
                link(b, dve.tensor_reduce(col(RANK), rk[:, :, :], AX_X, ALU.add))
                dve.tensor_scalar(col(KEEP), col(RANK), float(CAP), None, ALU.is_lt)
                link(b, dve.tensor_scalar(col(BASE), col(LAST), -float(CAP), float(SLOTS), ALU.mult, ALU.add))
                link(b, dve.tensor_tensor(col(KRANK), col(KEEP), col(RANK), ALU.mult))
                dve.tensor_tensor(wtok[:, b, :], col(PROB), col(KEEP), ALU.mult)
                link(b, dve.tensor_tensor(col(KRANK), col(BASE), col(KRANK), ALU.add))
                dve.tensor_copy(gidx[:, b, :], col(KRANK))
                link(b, dve.tensor_tensor(col(DIFF), col(KRANK), junk[:, :], ALU.subtract))
                link(b, dve.tensor_tensor(col(PICK), col(DIFF), col(KEEP), ALU.mult))
                dve.tensor_tensor(sidx[:, :], col(PICK), junk[:, :], ALU.add).then_inc(idx_ready, 1)
                link(b, dve.tensor_scalar(junk[:, :], junk[:, :], float(S), None, ALU.add))
                moved(dve, b, ("rank",))

            dve.wait_ge(d_cst, 16)
            dve.tensor_copy(cstb[:, :], cst[:, 0:4 * P]).then_inc(c_ready, 1)
            dve.tensor_copy(junk[:, :], cst[:, C_JUNK:C_JUNK + T]).then_inc(c_ready, 1)
            dve.wait_ge(c_ready, 4)
            dve.wait_ge(d_w, 16 * 11)
            with dve.Fori(0, B) as b:
                links[0] = 0
                dve.wait_ge(d_x, b * 16 + 16)
                dve.wait_ge(d_res, b * 16)
                norm_stats(b, xb)
                norm_apply(xb)
                for t in range(T):
                    rope(b, t)
                for n in range(4):
                    split(b, n)
                attend(b, 0)
                for half in range(2):
                    full(dve, b, ("vc", half))
                    src = bank(("vc", half)).rearrange("p (t h d) -> p t h d", t=2, h=H)
                    for i in range(2):
                        ins = dve.tensor_tensor(V["cross"][:, 2 * half + i, :, 0:HD], src[:, i, :, :],
                                                bv_sb[:, :].rearrange("p (h d) -> p h d", h=H), ALU.add)
                    moves(ins, ("vc", half))
                add_rows(b, "o", xb)
                norm_stats(b, x1)
                norm_apply(x1)
                split(b, 6)
                split(b, 7)
                attend(b, 1)
                add_rows(b, "xo", x1)
                norm_stats(b, x1)
                link(b, dve.tensor_tensor(rsq[:, :], rstd[:, :], rstd[:, :], ALU.mult))
                link(b, dve.tensor_tensor(var2[:, :], rsq[:, :], mv[:, :, 1], ALU.mult))
                rsqrt(b, rstd2[:, :], var2[:, :])
                norm_apply(x1)
                dve.wait_ge(xn_ready, b * (3 * T) + 3 * T)
                dve.wait_ge(d_scat, b * (16 * T))
                for t in range(T):
                    dve.scalar_tensor_tensor(out=tok[:, t, :], in0=xn[:, t, :], scalar=rstd2[:, t:t + 1], in1=gam_sb[:, :],
                                             op0=ALU.mult, op1=ALU.mult).then_inc(tokg_ready, 1)
                route(b)
                assert links[0] == N_CHAIN, links[0]

            with dve.Fori(0, E // 2) as u:
                for par in range(2):
                    dve.wait_ge(d_y[par], u * 16)
                    for half in range(2):
                        k = 2 * par + half
                        dve.wait_ge(y_full, u * 4 + k + 1)
                        dve.tensor_copy(yb[:, par, 2 * half:2 * half + 2, :],
                                        r_bank[half].rearrange("p (t d) -> p t d", t=2)).then_inc(y_free, 1)
            dve.wait_ge(d_rg, 16 * B)
            for n in range(16):
                dve.wait_ge(d_yg[n], 16)
                dve.scalar_tensor_tensor(out=rg[:, n, :], in0=yg[:, n, :], scalar=wtok[:, n // T, n % T:n % T + 1], in1=rg[:, n, :],
                                         op0=ALU.mult, op1=ALU.add).then_inc(o_ready, 1)
    return nc


def kernel(**inputs):
    import numpy as np
    import concourse.bacc as bacc
    from concourse import mybir as mb
    from concourse.bass_utils import run_bass_kernel_spmd

    f = np.float32

    def get(name):
        return np.asarray(inputs[name])

    def padded(w, b):
        rows = np.zeros((G, GH, 2 * HD, D), f)
        rows[:, :, 0:HD] = w.reshape(G, GH, HD, D)
        rows[0, 0, HD] = b
        return rows.reshape(G * P, D)

    consts = np.zeros((P, C_ALL), f)
    i = np.arange(P)
    consts[:, C_ID:C_ID + P] = i[:, None] == i[None, :]
    consts[:, C_PRE:C_PRE + P] = i[:, None] < i[None, :]
    consts[:, C_MQ:C_MQ + P] = np.where(i[None, :] > i[:, None], f(-1e30), f(0))
    consts[:, C_MK:C_MK + P] = np.where(i[:, None] > i[None, :], f(-1e30), f(0))
    consts[:, C_REV:C_REV + E] = E - np.arange(E)
    consts[:, C_JUNK:C_JUNK + T] = SLOTS + np.arange(T)[None, :] * P + i[:, None]
    freqs = f(1.0) / f(10000.0) ** (np.arange(HD // 2, dtype=f) / f(HD // 2))
    angle = (np.arange(S, dtype=f)[:, None] * freqs[None, :]).reshape(T, P, HD // 2).transpose(1, 0, 2)
    consts[:, C_COS:C_COS + T * HD] = np.repeat(np.cos(angle), 2, axis=2).reshape(P, T * HD)
    consts[:, C_SIN:C_SIN + T * HD] = np.stack([-np.sin(angle), np.sin(angle)], axis=3).reshape(P, T * HD)

    def rows(a):
        return np.ascontiguousarray(np.broadcast_to(a[None, :], (P, D)))

    bkv = get("L0_xattn_bkv")
    arrays = {
        "x": get("x"),
        "ctxT": get("ctx_768").transpose(0, 2, 1),
        "consts": consts,
        "wqkv": np.concatenate([get("L0_attn_Wq"), get("L0_attn_Wk"), get("L0_attn_Wv")], axis=1),
        "wo": padded(get("L0_attn_Wo"), get("L0_attn_bo")),
        "xwq": get("L0_xattn_Wq"),
        "xwkv": get("L0_xattn_Wkv"),
        "xwo": padded(get("L0_xattn_Wo"), get("L0_xattn_bo")),
        "bq": get("L0_xattn_bq").reshape(C, P).T,
        "bk": bkv[0:D].reshape(C, P).T,
        "bv": rows(bkv[D:2 * D]),
        "gamma": rows(get("L0_ffn_ln_gamma")),
        "beta": rows(get("L0_ffn_ln_beta")),
        "gateT": get("L0_ffn_gate_weight").T,
        "wi": get("L0_ffn_wi"),
        "wo_e": get("L0_ffn_wo"),
    }
    arrays = {k: np.ascontiguousarray(a) for k, a in arrays.items()}
    nc = bacc.Bacc("TRN2", target_bir_lowering=False, num_devices=1)
    args = [nc.dram_tensor("in_" + k, a.shape, mb.dt.from_np(a.dtype), kind="ExternalInput").ap() for k, a in arrays.items()]
    args.append(nc.dram_tensor("out_0", (B, S, D), F32, kind="ExternalOutput").ap())
    build(nc, *args)
    r = run_bass_kernel_spmd(nc, [{"in_" + k: a for k, a in arrays.items()}], core_ids=[0])
    return r.results[0]["out_0"]
```

```python
from contextlib import ExitStack

import concourse.bass as bass
from concourse import mybir

P = 128
F32 = mybir.dt.float32
BF16 = mybir.dt.bfloat16
I32 = mybir.dt.int32
ALU = mybir.AluOpType
ACT = mybir.ActivationFunctionType
AX_X = mybir.AxisListType.X

B, S, D = 4, 512, 256
DC = 192
H, HD = 16, 16
E, I, CAP = 8, 1024, 512
N_TOK = B * S
T = S // P
C = D // P
CK = DC // 2
G, GH = 4, 4
IC = I // P
EPS = 1e-5
SCALE = HD ** -0.5
SLOTS = E * CAP

Q_PARTS = (0, 0, 0, 1, 1, 2)
K_PARTS = (0, 1, 2, 0, 1, 0)
SROWS = HD * len(Q_PARTS)
XROWS = SROWS + 2

C_ID, C_PRE, C_MQ, C_MK, C_REV, C_JUNK, C_COS, C_SIN = 0, 128, 256, 384, 512, 520, 524, 588
C_ALL = C_SIN + T * HD


QK_USE, V_USE = (0, 1, 3, 4), (2, 5)
JOBS = [(0, 0, g) for g in range(G)] + [(0, 1, g) for g in range(G)] + [None, None] + \
       [(1, 0, g) for g in range(G)] + [(1, 1, g) for g in range(G)]
REAL = [j for j in JOBS if j is not None]
CREDIT_MAX = {(p, g): int((1, p, g) in REAL[-2:]) for p in range(2) for g in range(G)}
STEPS = len(JOBS) + 3
AHEAD = [("lnx", 0), ("xT", 0), ("qkv", 0), ("rT", 0), ("lnx", 1)]
FILL = {
    ("end", 0): [("xT", 1)], ("end", 1): [("qkv", 1)], ("end", 2): [("rT", 1)],
    ("end", 7): [("oT", 0, 0), ("kc", 0), ("vc", 0), ("o", 0, 0), ("lny", 0)],
    ("end", 8): [("yT", 0)], ("mid", 9): [("qc", 0)],
    ("end", 10): [("kc", 1), ("vc", 1)],
    ("end", 11): [("oT", 1, 0)], ("mid", 12): [("o", 1, 0), ("lny", 1)],
    ("end", 12): [("yT", 1)], ("mid", 13): [("qc", 1)],
    ("end", 17): [("oT", 0, 1)], ("mid", 18): [("o", 0, 1), ("fin", 0)],
    ("end", 19): [("tT", 0), ("logit", 0)], ("mid", 20): [("rank", 0)],
    ("end", 20): [("oT", 1, 1), ("o", 1, 1), ("fin", 1), ("tT", 1), ("logit", 1), ("rank", 1)],
}
SPLIT_KINDS = ("rT", "kc", "qc")
USES_OF = {"xT": 2, "qkv": 6, "rT": 4, "kc": 2, "vc": 2, "oT": 2, "o": 2, "yT": 2, "qc": 2, "tT": 2, "logit": 1, "rank": 1}
S_USES = ([(h, tiles) for h in range(GH) for tiles in ((3,), (0, 2), (1,))],
          [(h, (q,)) for h in range(GH) for q in range(T)])


def job(i):
    return JOBS[i] if 0 <= i < len(JOBS) else None


def walk():
    for f in AHEAD:
        yield ("fill", f)
    for i in range(STEPS):
        for q in range(T):
            yield ("quarter", i, q)
            if q == 2:
                for f in FILL.get(("mid", i), ()):
                    yield ("fill", f)
        yield ("close", i)
        for f in FILL.get(("end", i), ()):
            yield ("fill", f)


class Counts:

    def __init__(self):
        self.ring, self.score, self.exp, self.split = {}, {}, {}, {}
        for w in walk():
            if w[0] == "fill":
                for n in range(USES_OF.get(w[1][0], 0)):
                    self.ring[w[1] + (n,)] = len(self.ring)
                    if w[1][0] in SPLIT_KINDS:
                        self.split[w[1] + (n,)] = len(self.split)
            elif w[0] == "quarter":
                _, i, q = w
                if job(i - 3) and q == 0:
                    self.ring[("pv", job(i - 3))] = len(self.ring)
                if job(i):
                    for n in range(4 * q, min(4 * q + 4, len(S_USES[job(i)[0]]))):
                        self.score[job(i), n] = len(self.score)
                if job(i - 2):
                    for pair in range(2):
                        self.exp[job(i - 2), q, pair] = len(self.exp)
                if job(i - 1) and q == 0:
                    self.ring[("max", job(i - 1))] = len(self.ring)
                if job(i - 3) and q == 2:
                    self.ring[("ot", job(i - 3))] = len(self.ring)
        assert not any(len(c) % 2 for c in (self.ring, self.score, self.exp, self.split)), [len(c) for c in (self.ring, self.score, self.exp, self.split)]


def build(nc, x, ctxT, consts, wqkv, wo, xwq, xwkv, xwo, bq, bk, rows5, gateT, wi, wo_e, out):
    cnt = Counts()
    NR, NS, NE, NSPL = len(cnt.ring) // 2, len(cnt.score), len(cnt.exp), len(cnt.split)
    NJ = len(REAL)
    TURNS = B // 2

    spill = nc.dram_tensor("spill", [2, 3, P, S], BF16, kind="Internal")
    disp = nc.dram_tensor("disp", [SLOTS + N_TOK, D], F32, kind="Internal")
    ydram = nc.dram_tensor("ydram", [SLOTS, D], F32, kind="Internal")
    resid = nc.dram_tensor("resid", [B, S, D], F32, kind="Internal")

    with ExitStack() as stack:
        def sb(name, shape, dt=F32):
            return stack.enter_context(nc.sbuf_tensor(name, shape, dt))

        def sem(name):
            return stack.enter_context(nc.semaphore(name))

        def two(name):
            return [sem(name + "0"), sem(name + "1")]

        cst = sb("cst", [P, C_ALL])
        cosT = cst[:, C_COS:C_COS + T * HD].rearrange("p (t d) -> p t d", t=T)
        sinT = cst[:, C_SIN:C_SIN + T * HD].rearrange("p (t d) -> p t d", t=T)
        identf = cst[:, C_ID:C_ID + P]
        cstb = sb("cstb", [P, 4 * P], BF16)
        identb, prefb, maskqb, maskkb = (cstb[:, n * P:(n + 1) * P] for n in range(4))
        onesb = sb("onesb", [P, P], BF16)
        wqkv_sb = sb("wqkv_sb", [P, C, 3 * D])
        wo_sb = [sb("wo_sb", [P, C, D]), sb("xwo_sb", [P, C, D])]
        xwq_sb = sb("xwq_sb", [P, C, D])
        xwkv_sb = sb("xwkv_sb", [CK, 2, 2 * D])
        bq_sb = sb("bq_sb", [P, C])
        bk_sb = sb("bk_sb", [P, C])
        rows_sb = sb("rows_sb", [P, 5, D])
        bo_sb = [rows_sb[:, 0, :], rows_sb[:, 1, :]]
        bv_sb, gam_sb, bet_sb = (rows_sb[:, n, :] for n in (2, 3, 4))
        gate_sb = sb("gate_sb", [P, C, E])

        xb = [sb("xb0", [P, T, D]), sb("xb1", [P, T, D])]
        xn = [sb("xn0", [P, T, D]), sb("xn1", [P, T, D])]
        tok = sb("tok", [P, T, D])
        xnT = sb("xnT", [P, C, S])
        ctx_sb = sb("ctx_sb", [CK, 2, S])
        rc = sb("rc", [P, 2, 2 * D])
        rs = sb("rs", [P, 2, 2 * D])
        rot = sb("rot", [P, T, 2 * D])
        att = [rot[:, :, p * D:(p + 1) * D] for p in range(2)]
        attT = sb("attT", [P, C, S])
        pv_sb = sb("pv_sb", [P, S])
        src32 = sb("src32", [P, 2, S])
        rem32 = sb("rem32", [P, 2, S])
        parts = sb("parts", [P, 2, 3, S], BF16)
        V = [sb("v0", [P, T, H, 2 * HD]), sb("v1", [P, T, H, 2 * HD])]
        rsum = sb("rsum", [P, 2, T, GH])
        mx = sb("mx", [P, 2, GH, T])
        nmx = sb("nmx", [P, 2, 2, GH * T], BF16)
        mrow = sb("mrow", [2 * GH * T, 2, P], BF16)
        stats = sb("stats", [P, T, 6])
        mv = sb("mv", [P, T, 2])
        rstd = sb("rstd", [P, T])
        rsq = sb("rsq", [P, T])
        newton = sb("newton", [P, 2, T])
        var2 = sb("var2", [P, T])
        rstd2 = sb("rstd2", [P, T])
        z = sb("z", [P, T, E])
        ez = sb("ez", [P, T, E])
        cand = sb("cand", [P, T, E])
        onehot = sb("onehot", [P, T, E])
        onehotb = sb("onehotb", [P, T, E], BF16)
        rk = sb("rk", [P, T, E])
        count = sb("count", [P, E])
        small = sb("small", [P, 12, T])
        junk = sb("junk", [P, T])
        sidx = sb("sidx", [P, T], I32)
        gidx = sb("gidx", [P, B, T], I32)
        wtok = sb("wtok", [P, B, T])
        slab = sb("slab", [P, 8192 + 4 * 4096])
        prob = slab[:, 0:8192].rearrange("p (t h s) -> p t h s", t=T, h=GH)
        o = 8192

        def stack_view():
            nonlocal o
            o += 4096
            return slab[:, o - 4096:o].bitcast(BF16).rearrange("p (h s) -> p h s", h=H)
        qst = [stack_view(), stack_view()]
        kst = [stack_view(), stack_view()]
        o = 0

        def carve(n):
            nonlocal o
            o += n
            return slab[:, o - n:o]
        woe_sb = carve(2 * IC * D).rearrange("p (b c d) -> p b c d", b=2, c=IC)
        wi_sb = carve(2 * C * I).rearrange("p (b c d) -> p b c d", b=2, c=C)
        hT = carve(IC * CAP).rearrange("p (c s) -> p c s", c=IC)
        dsp = carve(2 * T * D).rearrange("p (b t d) -> p b t d", b=2, t=T)
        dspT = carve(2 * C * CAP).rearrange("p (b c s) -> p b c s", b=2, c=C)
        yb = carve(2 * T * D).rearrange("p (b t d) -> p b t d", b=2, t=T)
        yg = hT.rearrange("p c s -> p (c s)").rearrange("p (n d) -> p n d", n=16)
        rg = slab[:, o - 16 * D:o].rearrange("p (n d) -> p n d", n=16)

        ps = stack.enter_context(nc.psum_tensor("ps", [P, 8, S], F32))
        s_bank = [ps[:, n, :] for n in (0, 1)]
        e_bank = [ps[:, 2:4, :], ps[:, 4:6, :]]
        r_bank = [ps[:, n, :] for n in (6, 7)]

        d_cst, d_w, d_ctx, d_out, d_zero = (sem(n) for n in ("d_cst", "d_w", "d_ctx", "d_out", "d_zero"))
        d_x = two("d_x")
        c_ready, v_ready, z_ready = sem("c_ready"), sem("v_ready"), sem("z_ready")
        ring_full = two("ring_full")
        ring_moved = two("ring_moved")
        xn_ready = sem("xn_ready")
        bias_ready = sem("bias_ready")
        rot_ready = sem("rot_ready")
        hi_ready, mid_ready = sem("hi_ready"), sem("mid_ready")
        rem_ready, lo_ready = sem("rem_ready"), sem("lo_ready")
        d_spill = two("d_spill")
        d_q = [[sem(f"d_q{p}{c}") for c in range(C)] for p in range(2)]
        d_k = [[sem(f"d_k{p}{c}") for c in range(C)] for p in range(2)]
        s_full, s_free = sem("s_full"), sem("s_free")
        mx_ready = sem("mx_ready")
        d_max = [[sem(f"d_max{p}{g}") for g in range(G)] for p in range(2)]
        e_full, e_done = sem("e_full"), sem("e_done")
        res_ready, d_res = sem("res_ready"), two("d_res")
        tokg_ready, tok_ready = sem("tokg_ready"), sem("tok_ready")
        ez_ready, oh_ready = sem("ez_ready"), sem("oh_ready")
        idx_ready, d_scat = sem("idx_ready"), sem("d_scat")
        chain = sem("chain")
        tok_free = sem("tok_free")
        held, held_pool = sem("held"), sem("held_pool")
        t_full, t_free, h_full, h_free, y_full, y_free = (sem(n) for n in ("t_full", "t_free", "h_full", "h_free", "y_full", "y_free"))
        d_wi, d_wo, d_dsp, d_y = two("d_wi"), two("d_wo"), two("d_dsp"), two("d_y")
        d_rg, d_yg = sem("d_rg"), [sem(f"d_yg{n}") for n in range(16)]
        o_ready = sem("o_ready")

        N_CHAIN = 174

        block = stack.enter_context(nc.Block())

        def wait_credit(eng, s, value):
            eng.wait_ge(s, value + 1)

        def full(eng, u, name):
            n = cnt.ring[name]
            eng.wait_ge(ring_full[n % 2], u * NR + n // 2 + 1)

        def bank(name):
            return r_bank[cnt.ring[name] % 2]

        def filled(ins, name):
            ins.then_inc(ring_full[cnt.ring[name] % 2], 1)

        def moved(eng, u, *names):
            for n in (0, 1):
                counts = [cnt.ring[name] // 2 + 1 for name in names if cnt.ring[name] % 2 == n]
                if counts:
                    wait_credit(eng, ring_moved[n], u * NR + max(counts))

        def moves(ins, name):
            ins.then_inc(ring_moved[cnt.ring[name] % 2], 1)

        @block.sync
        def _(sp):
            def stack_job(u, f, n, stk, c, done):
                k = cnt.split[f + (n,)]
                par = k % 2
                sp.wait_ge(lo_ready, u * NSPL + k + 1)
                sp.dma_start(spill[par].rearrange("j p n -> p j n"), parts[:, par, :, :]).then_inc(d_spill[par], 16)
                wait_credit(sp, d_spill[par], u * (8 * NSPL) + 16 * (k // 2 + 1))
                for i, j in enumerate(Q_PARTS if stk in qst else K_PARTS):
                    sp.dma_start(stk[16 * i:16 * i + 16, 8 * c:8 * c + 8, :],
                                 spill[par, j].rearrange("(h d) n -> d h n", h=8)).then_inc(done, 16)

            def max_job(u, j):
                a, p, g = j
                k = REAL.index(j)
                moved(sp, u, ("max", j))
                for part in range(2):
                    sp.dma_start(qst[p][SROWS + part:SROWS + part + 1, GH * g:GH * g + GH, :].rearrange("p h (t c) -> p (h t) c", c=P),
                                 mrow[16 * part:16 * part + 16, k % 2, :]).then_inc(d_max[p][g], 16)

            def load_ctx(u, p):
                sp.dma_start(ctx_sb[:, :, :], ctxT[u * 2 + p].rearrange("(c p) n -> p c n", p=CK)).then_inc(d_ctx, 16)

            def fill(u, f):
                kind, p = f[0:2]
                if kind == "rT":
                    for n, (stk, sems, c) in enumerate(((qst, d_q, 0), (kst, d_k, 0), (qst, d_q, 1), (kst, d_k, 1))):
                        stack_job(u, f, n, stk[p], c, sems[p][c])
                if kind == "kc":
                    for c in range(C):
                        stack_job(u, f, c, kst[p], c, d_k[p][c])
                if kind == "qc":
                    for c in range(C):
                        stack_job(u, f, c, qst[p], c, d_q[p][c])
                if kind == "vc" and p == 0:
                    full(sp, u, ("vc", 0, 1))
                    load_ctx(u, 1)
                if kind == "rank":
                    sp.wait_ge(res_ready, u * 2 + p + 1)
                    sp.dma_start(resid[u * 2 + p].rearrange("(t p) d -> p t d", p=P), xn[p][:, :, :]).then_inc(d_res[p], 16)

            sp.dma_start(cst[:, :], consts).then_inc(d_cst, 16)
            sp.dma_start(xb[0][:, :, :], x[0].rearrange("(t p) d -> p t d", p=P)).then_inc(d_x[0], 16)
            sp.dma_start(wqkv_sb[:, :, :], wqkv.rearrange("(c p) n -> p c n", p=P)).then_inc(d_w, 16)
            sp.dma_start(xb[1][:, :, :], x[1].rearrange("(t p) d -> p t d", p=P)).then_inc(d_x[1], 16)
            for dst, src in ((wo_sb[0], wo), (xwq_sb, xwq), (wo_sb[1], xwo), (gate_sb, gateT)):
                sp.dma_start(dst[:, :, :], src.rearrange("(c p) n -> p c n", p=P)).then_inc(d_w, 16)
            sp.dma_start(xwkv_sb[:, :, :], xwkv.rearrange("(c p) n -> p c n", p=CK)).then_inc(d_w, 16)
            sp.dma_start(bq_sb[:, :], bq).then_inc(d_w, 16)
            sp.dma_start(bk_sb[:, :], bk).then_inc(d_w, 16)
            sp.dma_start(rows_sb[:, :, :], rows5).then_inc(d_w, 16)
            sp.wait_ge(z_ready, 1)
            for n in range(E):
                sp.dma_start(disp[n * CAP:(n + 1) * CAP, :].rearrange("(t p) d -> p t d", p=P),
                             slab[:, 0:T * D].rearrange("p (t d) -> p t d", t=T)).then_inc(d_zero, 16)
            load_ctx(0, 0)
            with sp.Fori(0, TURNS) as u:
                for w in walk():
                    if w[0] == "fill":
                        fill(u, w[1])
                    if w[0] == "quarter" and w[2] == 1 and job(w[1] - 1):
                        max_job(u, job(w[1] - 1))
                for p in range(2):
                    sp.wait_ge(res_ready, u * 2 + 2)
                    sp.dma_start(xb[p][:, :, :], x[(u * 2 + (2 + p)) % B].rearrange("(t p) d -> p t d", p=P)).then_inc(d_x[p], 16)
                sp.dma_start(ctx_sb[:, :, :], ctxT[(u * 2 + 2) % B].rearrange("(c p) n -> p c n", p=CK)).then_inc(d_ctx, 16)

            def load_w(e, par):
                sp.dma_start(wi_sb[:, par, :, :], wi[e].rearrange("(c p) n -> p c n", p=P)).then_inc(d_wi[par], 16)
                sp.dma_start(woe_sb[:, par, :, :], wo_e[e].rearrange("(c p) n -> p c n", p=P)).then_inc(d_wo[par], 16)
                sp.dma_start(dsp[:, par, :, :], disp[bass.ds(e * CAP, CAP), :].rearrange("(t p) d -> p t d", p=P)).then_inc(d_dsp[par], 16)

            for s in ring_full:
                sp.wait_ge(s, TURNS * NR)
            sp.wait_ge(d_scat, B * T * 16)
            for par in range(2):
                load_w(par, par)
            with sp.Fori(0, E // 2) as u:
                for par in range(2):
                    wait_credit(sp, y_free, u * 4 + 2 * par + 2)
                    sp.dma_start(ydram[bass.ds(u * (2 * CAP) + par * CAP, CAP), :].rearrange("(t p) d -> p t d", p=P),
                                 yb[:, par, :, :]).then_inc(d_y[par], 16)
                    load_w((u * 2 + (par + 2)) % E, par)
            for par in range(2):
                wait_credit(sp, d_y[par], 8 * E)
            for b in range(B):
                sp.dma_start(rg[:, 4 * b:4 * b + 4, :], resid[b].rearrange("(t p) d -> p t d", p=P)).then_inc(d_rg, 16)
            for b in range(B):
                sp.wait_ge(o_ready, 4 * b + 4)
                sp.dma_start(out[b].rearrange("(t p) d -> p t d", p=P), rg[:, 4 * b:4 * b + 4, :]).then_inc(d_out, 16)
            sp.wait_ge(d_out, 16 * B)
            sp.wait_ge(d_ctx, 16 * (B + 1))
            for par in range(2):
                sp.wait_ge(d_x[par], 16 * (TURNS + 1))
                for d in (d_wi, d_wo, d_dsp):
                    sp.wait_ge(d[par], 8 * E + 16)

        @block.gpsimd
        def _(pool):
            pool.memset(slab[:, 0:T * D], 0.0).then_inc(z_ready, 1)
            pool.memset(onesb[:, :], 1.0).then_inc(c_ready, 1)
            pool.memset(count[:, :], 0.0).then_inc(c_ready, 1)
            for v in V:
                pool.memset(v[:, :, :, HD:2 * HD], 1.0).then_inc(v_ready, 1)
            pool.wait_ge(v_ready, 2)
            pool.memset(kst[0][SROWS:XROWS, :, :], 1.0).then_inc(v_ready, 1)
            pool.wait_ge(v_ready, 3)
            pool.memset(kst[1][SROWS:XROWS, :, :], 1.0).then_inc(v_ready, 1)
            pool.wait_ge(v_ready, 4)

            def rows_sent(batches):
                pool.wait_ge(d_scat, batches * (16 * T))
                pool.sem_inc(tok_free, 1)

            def add_bias(u, a, p, norms):
                pool.wait_ge(xn_ready, u * (6 * T) + norms * T)
                for t in range(T):
                    ins = pool.tensor_tensor(xb[p][:, t, :], xb[p][:, t, :], bo_sb[a], ALU.add)
                ins.then_inc(bias_ready, 1)

            def fill(u, f):
                kind, p = f[0:2]
                if kind == "lnx":
                    add_bias(u, 0, p, p + 1)
                if kind == "lny":
                    add_bias(u, 1, p, 3 + p)
                if kind == "qkv":
                    for t in range(T):
                        moved(pool, u, f + (QK_USE[t],))
                        pool.tensor_tensor(rot[:, t, :], rc[:, t % 2, :], rs[:, t % 2, :], ALU.add).then_inc(rot_ready, 1)
                if kind in SPLIT_KINDS:
                    for n in range(USES_OF[kind]):
                        k = cnt.split[f + (n,)]
                        par = k % 2
                        pool.wait_ge(hi_ready, u * NSPL + k + 1)
                        pool.tensor_tensor(rem32[:, par, :], src32[:, par, :], parts[:, par, 0, :], ALU.subtract).then_inc(rem_ready, 1)
                        pool.wait_ge(mid_ready, u * NSPL + k + 1)
                        pool.tensor_tensor(parts[:, par, 2, :], rem32[:, par, :], parts[:, par, 1, :], ALU.subtract).then_inc(lo_ready, 1)
                if kind == "fin":
                    for t in range(T):
                        pool.wait_ge(tokg_ready, (u * 2 + p) * T + t + 1)
                        pool.tensor_tensor(tok[:, t, :], tok[:, t, :], bet_sb, ALU.add).then_inc(tok_ready, 1)
                    pool.tensor_tensor(xn[p][:, :, :], xn[p][:, :, :], xb[p][:, :, :], ALU.add).then_inc(res_ready, 1)
                if kind == "rank":
                    pool.wait_ge(idx_ready, u * 2 + p + 1)
                    pool.sem_inc(held_pool, 1)
                    pool.wait_ge(d_zero, 16 * E)
                    for t in range(T):
                        pool.indirect_dma_start(disp[:, :], bass.IndirectOffsetOnAxis(ap=sidx[:, t:t + 1], axis=0),
                                                tok[:, t, :], None).then_inc(d_scat, 16)
                if f == ("o", 1, 1):
                    rows_sent(u * 2 + 1)

            pool.wait_ge(d_w, 16 * 9)
            with pool.Fori(0, TURNS) as u:
                for w in walk():
                    if w[0] == "fill":
                        fill(u, w[1])
                rows_sent(u * 2 + 2)
            for par in range(2):
                wait_credit(pool, d_y[par], 8 * E)
            for n in range(16):
                pool.indirect_dma_start(yg[:, n, :], None, ydram[:, :],
                                        bass.IndirectOffsetOnAxis(ap=gidx[:, n // T, n % T:n % T + 1], axis=0)).then_inc(d_yg[n], 16)

        @block.scalar
        def _(act):
            def move(u, name, dst, func=ACT.Copy, src=None, **kw):
                full(act, u, name)
                moves(act.activation(dst, bank(name) if src is None else src, func, **kw), name)

            def exps(u, j, kt):
                q0 = kt * P if j[0] == 0 else 0
                for pair in range(2):
                    n = cnt.exp[j, kt, pair]
                    act.wait_ge(e_full, u * NE + n + 1)
                    act.activation(prob[:, kt, 2 * pair:2 * pair + 2, q0:S], e_bank[n % 2][:, :, q0:S], ACT.Exp,
                                   scale=SCALE).then_inc(e_done, 1)

            def fill(u, f):
                kind, p = f[0:2]
                if kind in ("xT", "yT", "tT"):
                    for c in range(C):
                        move(u, f + (c,), xnT[:, c, :])
                if kind == "oT":
                    for c in range(C):
                        move(u, f + (c,), attT[:, c, :])
                if kind == "qkv":
                    for half in range(2):
                        name = f + (V_USE[half],)
                        move(u, name, V[p][:, 2 * half:2 * half + 2, :, 0:HD], src=bank(name).rearrange("p (t h d) -> p t h d", t=2, h=H))
                if kind in SPLIT_KINDS:
                    bias = {"kc": bk_sb, "qc": bq_sb}.get(kind)
                    for n in range(USES_OF[kind]):
                        k = cnt.split[f + (n,)]
                        wait_credit(act, rem_ready, u * NSPL + (k - 1 if k >= 2 else 0))
                        if bias is None:
                            move(u, f + (n,), src32[:, k % 2, :])
                        else:
                            move(u, f + (n,), src32[:, k % 2, :], ACT.Identity, bias=bias[:, n:n + 1])
                if kind == "logit":
                    moved(act, u, f + (0,))
                    act.activation(ez[:, :, :], z[:, :, :], ACT.Exp).then_inc(ez_ready, 1)

            act.sem_inc(rem_ready, 1)
            act.wait_ge(d_w, 16 * 9)
            act.wait_ge(d_zero, 16 * E)
            with act.Fori(0, TURNS) as u:
                for w in walk():
                    if w[0] == "fill":
                        fill(u, w[1])
                    elif w[0] == "quarter":
                        _, i, q = w
                        if job(i - 3) and q == 1:
                            move(u, ("pv", job(i - 3)), pv_sb[:, :])
                        if job(i - 2):
                            exps(u, job(i - 2), q)
            with act.Fori(0, E // 2) as u:
                for par in range(2):
                    for c in range(C):
                        act.wait_ge(t_full, u * 4 + par * 2 + c + 1)
                        act.activation(dspT[:, par, c, :], s_bank[c], ACT.Copy).then_inc(t_free, 1)
                    for n in range(IC):
                        act.wait_ge(h_full, u * (2 * IC) + par * IC + n + 1)
                        act.activation(hT[:, n, :], ps[:, 2 + n % 4, :], ACT.Gelu).then_inc(h_free, 1)

        @block.tensor
        def _(pe):
            def take(u, name, *reads):
                for n in (0, 1):
                    counts = [cnt.ring[r] // 2 + 1 for r in reads if cnt.ring[r] % 2 == n]
                    counts += [cnt.ring[name] // 2] * (cnt.ring[name] % 2 == n)
                    if counts:
                        wait_credit(pe, ring_moved[n], u * NR + max(counts))
                return bank(name)

            def turn(u, name, src, ready=None, value=None, reads=()):
                dst = take(u, name, *reads)
                for t in range(T):
                    if ready is not None:
                        pe.wait_ge(ready, value + t + 1)
                    mm = pe.transpose(dst[:, t * P:(t + 1) * P], src(t), identf)
                filled(mm, name)

            def product(dst, n_chunks, lhsT, rhs):
                for c in range(n_chunks):
                    mm = pe.matmul(dst, lhsT(c), rhs(c), start=(c == 0), stop=(c == n_chunks - 1))
                return mm

            def score(u, j, n):
                a, p, g = j
                hh, tiles = S_USES[a][n]
                h = GH * g + hh
                k = cnt.score[j, n]
                wait_credit(pe, s_free, u * NS + (k - 1 if k else 0))
                dst, o = s_bank[k % 2], 0
                for qt in tiles:
                    w = (qt + 1) * P if a == 0 else S
                    mm = pe.matmul(dst[:, o:o + w], qst[p][0:SROWS, h, qt * P:(qt + 1) * P], kst[p][0:SROWS, h, 0:w],
                                   start=True, stop=True)
                    if a == 0:
                        mm = pe.matmul(dst[:, o + w - P:o + w], identb, maskqb, start=False, stop=True, skip_group_check=True)
                    o += w
                mm.then_inc(s_full, 1)

            def score_T(u, j, kt, pair):
                a, p, g = j
                n = cnt.exp[j, kt, pair]
                wait_credit(pe, e_done, u * NE + (n - 1 if n else 0))
                q0 = kt * P if a == 0 else 0
                for i in range(2):
                    h = GH * g + 2 * pair + i
                    dst = e_bank[n % 2][:, i, :]
                    mm = pe.matmul(dst[:, q0:S], kst[p][0:XROWS, h, kt * P:(kt + 1) * P], qst[p][0:XROWS, h, q0:S], start=True, stop=True)
                    if a == 0:
                        mm = pe.matmul(dst[:, q0:q0 + P], identb, maskkb, start=False, stop=True, skip_group_check=True)
                mm.then_inc(e_full, 1)

            def values(u, j, kt):
                a, p, g = j
                name = ("pv", j)
                dst = take(u, name) if kt == 0 else bank(name)
                wait_credit(pe, e_done, u * NE + cnt.exp[j, kt, 1] + 1)
                q0 = kt * P if a == 0 else 0
                for i in range(GH):
                    mm = pe.matmul(dst[32 * i:32 * i + 32, q0:S], V[p][:, kt, GH * g + i, :], prob[:, kt, i, q0:S],
                                   start=(kt == 0), stop=True, skip_group_check=True)
                if kt == T - 1:
                    filled(mm, name)

            def turn_max(u, j):
                name = ("max", j)
                k = REAL.index(j)
                dst = take(u, name).bitcast(BF16)
                pe.wait_ge(mx_ready, u * NJ + k + 1)
                filled(pe.transpose(dst[0:2 * GH * T, 0:P], nmx[:, k % 2, :, :].rearrange("p j n -> p (j n)"), identb), name)

            def quarter(u, i, q):
                j = job(i)
                if j and q % 2 == 0 and (q == 0 or len(S_USES[j[0]]) > 4 * q):
                    if q == 0 and j[2] % 2 == 0:
                        a, p, g = j
                        for d in (d_q, d_k):
                            pe.wait_ge(d[p][g // 2], u * 192 + a * 96 + 96)
                        if g == 0:
                            moved(pe, u, *((("qkv", p, n) for n in V_USE) if a == 0 else (("vc", p, n) for n in range(2))))
                for n in range(4 * q, 4 * q + 4):
                    if q == 0 and job(i - 3):
                        values(u, job(i - 3), n)
                    if j and n < len(S_USES[j[0]]):
                        score(u, j, n)
                    if job(i - 2) and n % 2 == 0:
                        a, p, g = job(i - 2)
                        if n == 0:
                            pe.wait_ge(d_max[p][g], u * 64 + a * 32 + 32 + CREDIT_MAX[p, g])
                        score_T(u, job(i - 2), q, (n % 4) // 2)
                if q == 0 and job(i - 1):
                    turn_max(u, job(i - 1))
                if q == 2 and job(i - 3):
                    name = ("ot", job(i - 3))
                    turn(u, name, lambda t: pv_sb[:, t * P:(t + 1) * P], reads=(("pv", job(i - 3)),))

            def fill(u, f):
                kind, p = f[0:2]
                if kind in ("xT", "yT"):
                    norms = p if kind == "xT" else 2 + p
                    for c in range(C):
                        turn(u, f + (c,), lambda t: xn[p][:, t, c * P:(c + 1) * P], xn_ready, u * (6 * T) + norms * T)
                if kind == "tT":
                    for c in range(C):
                        turn(u, f + (c,), lambda t: tok[:, t, c * P:(c + 1) * P], tok_ready, (u * 2 + p) * T)
                if kind == "oT":
                    last = ("ot", (f[2], p, G - 1))
                    for c in range(C):
                        turn(u, f + (c,), lambda t: att[p][:, t, c * P:(c + 1) * P], reads=(last,))
                if kind == "qkv":
                    for half in range(2):
                        for t in (2 * half, 2 * half + 1):
                            name = f + (QK_USE[t],)
                            dst = take(u, name, ("xT", p, 0), ("xT", p, 1))
                            filled(product(dst, C, lambda c: xnT[:, c, t * P:(t + 1) * P], lambda c: wqkv_sb[:, c, 0:2 * D]), name)
                        name = f + (V_USE[half],)
                        dst = take(u, name)
                        for i in range(2):
                            t = 2 * half + i
                            mm = product(dst[:, i * D:(i + 1) * D], C, lambda c: xnT[:, c, t * P:(t + 1) * P],
                                         lambda c: wqkv_sb[:, c, 2 * D:3 * D])
                        filled(mm, name)
                if kind == "rT":
                    for n, j in enumerate((0, 2, 1, 3)):
                        turn(u, f + (n,), lambda t: rot[:, t, j * P:(j + 1) * P], rot_ready, (u * 2 + p) * T)
                if kind == "kc":
                    pe.wait_ge(d_ctx, (u * 2 + p) * 16 + 16)
                    for m in range(C):
                        dst = take(u, f + (m,))
                        filled(product(dst, 2, lambda c: xwkv_sb[:, c, m * P:(m + 1) * P], lambda c: ctx_sb[:, c, :]), f + (m,))
                if kind == "vc":
                    for half in range(2):
                        dst = take(u, f + (half,))
                        for i in range(2):
                            t = 2 * half + i
                            mm = product(dst[:, i * D:(i + 1) * D], 2, lambda c: ctx_sb[:, c, t * P:(t + 1) * P],
                                         lambda c: xwkv_sb[:, c, D:2 * D])
                        filled(mm, f + (half,))
                if kind == "o":
                    for half in range(2):
                        dst = take(u, f + (half,), ("oT", p, f[2], 0), ("oT", p, f[2], 1))
                        for i in range(2):
                            t = 2 * half + i
                            mm = product(dst[:, i * D:(i + 1) * D], C, lambda c: attT[:, c, t * P:(t + 1) * P],
                                         lambda c: wo_sb[f[2]][:, c, :])
                        filled(mm, f + (half,))
                if kind == "qc":
                    for m in range(C):
                        dst = take(u, f + (m,), ("yT", p, 0), ("yT", p, 1))
                        filled(product(dst, C, lambda c: xwq_sb[:, c, m * P:(m + 1) * P], lambda c: xnT[:, c, :]), f + (m,))
                if kind == "logit":
                    dst = take(u, f + (0,), ("tT", p, 0), ("tT", p, 1))
                    for t in range(T):
                        mm = product(dst[:, t * E:(t + 1) * E], C, lambda c: xnT[:, c, t * P:(t + 1) * P], lambda c: gate_sb[:, c, :])
                    filled(mm, f + (0,))
                if kind == "rank":
                    dst = take(u, f + (0,))
                    pe.wait_ge(oh_ready, u * 2 + p + 1)
                    oh = onehotb[:, :, :].rearrange("p t e -> p (t e)")
                    pe.matmul(dst[:, 0:T * E], prefb, oh, start=True, stop=True, skip_group_check=True)
                    for k in range(1, T):
                        pe.matmul(dst[:, k * E:T * E], onesb[:, :], oh[:, 0:(T - k) * E], start=False, stop=True, skip_group_check=True)
                    for t in range(T):
                        mm = pe.matmul(dst[:, T * E:(T + 1) * E], onesb[:, :], oh[:, t * E:(t + 1) * E], start=False,
                                       stop=True, skip_group_check=True)
                    filled(mm, f + (0,))

            for s in (*ring_moved, s_free, e_done, h_free, y_free, tok_free):
                pe.sem_inc(s, 1)
            pe.wait_ge(d_cst, 16)
            pe.wait_ge(c_ready, 4)
            pe.wait_ge(v_ready, 4)
            pe.wait_ge(d_w, 16 * 9)
            with pe.Fori(0, TURNS) as u:
                for w in walk():
                    if w[0] == "fill":
                        fill(u, w[1])
                    elif w[0] == "quarter":
                        quarter(u, w[1], w[2])

            def turn_slots(par, loads, used):
                pe.wait_ge(d_dsp[par], loads)
                for c in range(C):
                    if used is not None:
                        pe.wait_ge(t_free, used + c)
                    for t in range(T):
                        mm = pe.transpose(s_bank[c][:, t * P:(t + 1) * P], dsp[:, par, t, c * P:(c + 1) * P], identf)
                    mm.then_inc(t_full, 1)

            wait_credit(pe, s_free, TURNS * NS)
            turn_slots(0, 16, None)
            wait_credit(pe, e_done, TURNS * NE)
            for s in ring_moved:
                wait_credit(pe, s, TURNS * NR)
            with pe.Fori(0, E // 2) as u:
                for par in range(2):
                    pe.wait_ge(t_free, u * 4 + 2 * par + 2)
                    pe.wait_ge(d_wi[par], u * 16 + 16)
                    for n in range(IC):
                        k = par * IC + n
                        wait_credit(pe, h_free, u * (2 * IC) + max(k - 3, 0))
                        product(ps[:, 2 + n % 4, :], C, lambda c: wi_sb[:, par, c, n * P:(n + 1) * P],
                                lambda c: dspT[:, par, c, :]).then_inc(h_full, 1)
                    turn_slots(1 - par, (u + par) * 16 + 16, u * 4 + 2 * par + 1)
                    pe.wait_ge(d_wo[par], u * 16 + 16)
                    wait_credit(pe, h_free, u * (2 * IC) + (par + 1) * IC)
                    for half in range(2):
                        k = 2 * par + half
                        wait_credit(pe, y_free, u * 4 + max(k - 1, 0))
                        for i in range(2):
                            t = 2 * half + i
                            mm = product(r_bank[half][:, i * D:(i + 1) * D], IC, lambda n: hT[:, n, t * P:(t + 1) * P],
                                         lambda n: woe_sb[:, par, n, :])
                        mm.then_inc(y_full, 1)

        @block.vector
        def _(dve):
            links = [0]

            def hold():
                dve.sem_inc(held, 1)

            def link(u, ins, plain=False):
                links[0] += 1
                ins.then_inc(chain, 1)
                dve.wait_ge(chain, u * N_CHAIN + links[0])
                if plain:
                    hold()

            def rsqrt(u, dst, var):
                v, guess = newton[:, 0, :], newton[:, 1, :]
                link(u, dve.tensor_scalar(v, var, EPS, None, ALU.add))
                link(u, dve.tensor_scalar(guess.bitcast(I32), v.bitcast(I32), 1, None, ALU.logical_shift_right))
                link(u, dve.tensor_scalar(dst.bitcast(I32), guess.bitcast(I32), -1.0, float(0x5f3759df), ALU.mult, ALU.add))
                for _ in range(3):
                    link(u, dve.tensor_tensor(guess, dst, dst, ALU.mult))
                    link(u, dve.scalar_tensor_tensor(out=guess, in0=guess, scalar=-0.5, in1=v, op0=ALU.mult, op1=ALU.mult))
                    link(u, dve.scalar_tensor_tensor(out=dst, in0=guess, scalar=1.5, in1=dst, op0=ALU.add, op1=ALU.mult))

            def norm_stats(u, p):
                for t in range(T):
                    i = dve.bn_stats(stats[:, t, :], xb[p][:, t, :])
                link(u, i, plain=True)
                for t in range(T):
                    i = dve.bn_aggr(mv[:, t, :], stats[:, t, :])
                link(u, i)
                rsqrt(u, rstd[:, :], mv[:, :, 1])

            def norm_apply(p):
                for t in range(T):
                    dve.tensor_scalar(xn[p][:, t, :], xb[p][:, t, :], mv[:, t, 0:1], rstd[:, t:t + 1], ALU.subtract, ALU.mult).then_inc(xn_ready, 1)

            def rope(u, f, t):
                name = f + (QK_USE[t],)
                full(dve, u, name)
                if t >= 2:
                    dve.wait_ge(rot_ready, (u * 2 + f[1]) * T + t - 1)
                src = bank(name).rearrange("p (h d) -> p h d", d=HD)
                pr = src.rearrange("p h (i two) -> p h i two", two=2)
                o = rs[:, t % 2, :].rearrange("p (h i two) -> p h i two", h=2 * H, two=2)
                sn = sinT[:, t, :].rearrange("p (i two) -> p i two", two=2)
                dve.tensor_tensor(rc[:, t % 2, :].rearrange("p (h d) -> p h d", d=HD), src,
                                  cosT[:, t:t + 1, :].to_broadcast([P, 2 * H, HD]), ALU.mult)
                for k in range(2):
                    i = dve.tensor_tensor(o[:, :, :, k], pr[:, :, :, 1 - k],
                                          sn[:, :, k:k + 1].rearrange("p i o -> p o i").to_broadcast([P, 2 * H, HD // 2]),
                                          ALU.mult)
                moves(i, name)

            def split(u, f, n):
                k = cnt.split[f + (n,)]
                par = k % 2
                moved(dve, u, f + (n,))
                wait_credit(dve, d_spill[par], u * (8 * NSPL) + 16 * (k // 2))
                dve.tensor_copy(parts[:, par, 0, :], src32[:, par, :]).then_inc(hi_ready, 1)
                dve.wait_ge(rem_ready, u * NSPL + k + 2)
                dve.tensor_copy(parts[:, par, 1, :], rem32[:, par, :]).then_inc(mid_ready, 1)

            def maxima(u, j, n):
                a, p, g = j
                hh, tiles = S_USES[a][n]
                k = cnt.score[j, n]
                dve.wait_ge(s_full, u * NS + k + 1)
                o = 0
                for qt in tiles:
                    w = (qt + 1) * P if a == 0 else S
                    i = dve.tensor_reduce(mx[:, REAL.index(j) % 2, hh, qt:qt + 1], s_bank[k % 2][:, o:o + w], AX_X, ALU.max)
                    o += w
                i.then_inc(s_free, 1)

            def negate(u, j):
                par = REAL.index(j) % 2
                wait_credit(dve, s_free, u * NS + cnt.score[j, len(S_USES[j[0]]) - 1] + 1)
                m = mx[:, par, :, :].rearrange("p h t -> p (h t)")
                link(u, dve.tensor_scalar(nmx[:, par, 0, :], m, -1.0, None, ALU.mult))
                dve.scalar_tensor_tensor(out=nmx[:, par, 1, :], in0=m, scalar=-1.0, in1=nmx[:, par, 0, :],
                                         op0=ALU.mult, op1=ALU.subtract).then_inc(mx_ready, 1)

            def max_rows(u, j):
                k = REAL.index(j)
                full(dve, u, ("max", j))
                a, p, g = REAL[k - 2]
                dve.wait_ge(d_max[p][g], u * 64 + (a * 32 + 32 if k >= 2 else 0) + CREDIT_MAX[p, g])
                moves(dve.tensor_copy(mrow[:, k % 2, :], bank(("max", j)).bitcast(BF16)[0:2 * GH * T, 0:P]), ("max", j))

            def normalise(u, j):
                a, p, g = j
                k = REAL.index(j) % 2
                full(dve, u, ("ot", j))
                src = bank(("ot", j)).rearrange("p (t h d) -> p t h d", t=T, h=GH)
                link(u, dve.reciprocal(rsum[:, k, :, :], src[:, :, :, HD:HD + 1].rearrange("p t h o -> p t (h o)")))
                for t in range(T):
                    i = dve.tensor_tensor(att[p][:, t, g * GH * HD:(g + 1) * GH * HD].rearrange("p (h d) -> p h d", h=GH), src[:, t, :, 0:HD],
                                          rsum[:, k, t, :].rearrange("p (h o) -> p h o", o=1).to_broadcast([P, GH, HD]), ALU.mult)
                moves(i, ("ot", j))

            def route_logits(u, f):
                full(dve, u, f + (0,))
                logit = bank(f + (0,))[:, 0:T * E].rearrange("p (t e) -> p t e", t=T)
                link(u, dve.tensor_reduce(col(TOP), logit, AX_X, ALU.max))
                moves(dve.tensor_tensor(z[:, :, :], logit, wide(TOP), ALU.subtract), f + (0,))
                moved(dve, u, f + (0,))
                link(u, dve.scalar_tensor_tensor(out=cand[:, :, :], in0=z[:, :, :], scalar=0.0, in1=rev, op0=ALU.is_ge, op1=ALU.mult))
                link(u, dve.tensor_reduce(col(LAST), cand[:, :, :], AX_X, ALU.max))
                link(u, dve.tensor_tensor(onehot[:, :, :], rev, wide(LAST), ALU.is_equal))
                dve.tensor_copy(onehotb[:, :, :], onehot[:, :, :]).then_inc(oh_ready, 1)
                dve.wait_ge(ez_ready, u * 2 + f[1] + 1)
                link(u, dve.tensor_reduce(col(DEN), ez[:, :, :], AX_X, ALU.add))
                link(u, dve.reciprocal(col(PROB), col(DEN)))

            def col(k):
                return small[:, k, :]

            def wide(k):
                return small[:, k, :].rearrange("p (t o) -> p t o", o=1).to_broadcast([P, T, E])

            rev = cst[:, C_REV:C_REV + E].rearrange("p (o e) -> p o e", o=1).to_broadcast([P, T, E])
            TOP, LAST, DEN, PROB, RANK, KEEP, BASE, KRANK, DIFF, PICK = range(10)

            def route_ranks(u, f):
                b = u * 2 + f[1]
                full(dve, u, f + (0,))
                pr = bank(f + (0,))
                link(u, dve.tensor_tensor(rk[:, :, :], pr[:, 0:T * E].rearrange("p (t e) -> p t e", t=T),
                                          count[:, :].rearrange("p (o e) -> p o e", o=1).to_broadcast([P, T, E]), ALU.add))
                moves(dve.tensor_tensor(count[:, :], pr[:, T * E:(T + 1) * E], count[:, :], ALU.add), f + (0,))
                link(u, dve.tensor_tensor(rk[:, :, :], rk[:, :, :], onehot[:, :, :], ALU.mult))
                link(u, dve.tensor_reduce(col(RANK), rk[:, :, :], AX_X, ALU.add))
                dve.tensor_scalar(col(KEEP), col(RANK), float(CAP), None, ALU.is_lt)
                link(u, dve.tensor_scalar(col(BASE), col(LAST), -float(CAP), float(SLOTS), ALU.mult, ALU.add))
                link(u, dve.tensor_tensor(col(KRANK), col(KEEP), col(RANK), ALU.mult))
                dve.tensor_tensor(wtok[:, b, :], col(PROB), col(KEEP), ALU.mult)
                link(u, dve.tensor_tensor(col(KRANK), col(BASE), col(KRANK), ALU.add))
                dve.tensor_copy(gidx[:, b, :], col(KRANK))
                link(u, dve.tensor_tensor(col(DIFF), col(KRANK), junk[:, :], ALU.subtract))
                link(u, dve.tensor_tensor(col(PICK), col(DIFF), col(KEEP), ALU.mult))
                dve.tensor_tensor(sidx[:, :], col(PICK), junk[:, :], ALU.add).then_inc(idx_ready, 1)
                link(u, dve.tensor_scalar(junk[:, :], junk[:, :], float(S), None, ALU.add))
                moved(dve, u, f + (0,))

            def fill(u, f):
                kind, p = f[0:2]
                if kind == "lnx":
                    dve.wait_ge(d_x[p], u * 16 + 16)
                    wait_credit(dve, d_res[p], u * 16)
                    norm_stats(u, p)
                    norm_apply(p)
                if kind == "lny":
                    norm_stats(u, p)
                    norm_apply(p)
                if kind == "qkv":
                    for t in range(T):
                        rope(u, f, t)
                if kind in SPLIT_KINDS:
                    for n in range(USES_OF[kind]):
                        split(u, f, n)
                if kind == "vc":
                    for half in range(2):
                        name = f + (half,)
                        full(dve, u, name)
                        src = bank(name).rearrange("p (t h d) -> p t h d", t=2, h=H)
                        for i in range(2):
                            ins = dve.tensor_tensor(V[p][:, 2 * half + i, :, 0:HD], src[:, i, :, :],
                                                    bv_sb.rearrange("p (h d) -> p h d", h=H), ALU.add)
                        moves(ins, name)
                if kind == "o":
                    dve.wait_ge(bias_ready, u * 4 + (p + 1 if f[2] == 0 else p + 3))
                    for half in range(2):
                        name = f + (half,)
                        full(dve, u, name)
                        rows = xb[p][:, 2 * half:2 * half + 2, :]
                        moves(dve.tensor_tensor(rows, bank(name).rearrange("p (t d) -> p t d", t=2), rows, ALU.add), name)
                    moved(dve, u, f + (0,), f + (1,))
                if kind == "fin":
                    norm_stats(u, p)
                    link(u, dve.tensor_tensor(rsq[:, :], rstd[:, :], rstd[:, :], ALU.mult))
                    link(u, dve.tensor_tensor(var2[:, :], rsq[:, :], mv[:, :, 1], ALU.mult))
                    rsqrt(u, rstd2[:, :], var2[:, :])
                    norm_apply(p)
                    dve.wait_ge(xn_ready, u * (6 * T) + (5 + p) * T)
                    wait_credit(dve, tok_free, u * 2 + p)
                    for t in range(T):
                        dve.scalar_tensor_tensor(out=tok[:, t, :], in0=xn[p][:, t, :], scalar=rstd2[:, t:t + 1], in1=gam_sb,
                                                 op0=ALU.mult, op1=ALU.mult).then_inc(tokg_ready, 1)
                if kind == "logit":
                    route_logits(u, f)
                if kind == "rank":
                    route_ranks(u, f)

            for s in (*d_spill, *d_res, *d_y, *(d_max[REAL[k][1]][REAL[k][2]] for k in (-2, -1))):
                dve.sem_inc(s, 1)
            dve.wait_ge(d_cst, 16)
            dve.tensor_copy(cstb[:, :], cst[:, 0:4 * P]).then_inc(c_ready, 1)
            dve.tensor_copy(junk[:, :], cst[:, C_JUNK:C_JUNK + T]).then_inc(c_ready, 1)
            dve.wait_ge(c_ready, 4)
            dve.wait_ge(d_w, 16 * 9)
            with dve.Fori(0, TURNS) as u:
                links[0] = 0
                for w in walk():
                    if w[0] == "fill":
                        fill(u, w[1])
                    elif w[0] == "quarter":
                        _, i, q = w
                        for n in range(4 * q, 4 * q + 4):
                            if job(i) and n < len(S_USES[job(i)[0]]):
                                maxima(u, job(i), n)
                            if n == 5 and job(i - 1):
                                max_rows(u, job(i - 1))
                            if n == 11 and job(i - 3):
                                normalise(u, job(i - 3))
                    elif w[0] == "close" and job(w[1]):
                        negate(u, job(w[1]))
                assert links[0] == N_CHAIN, links[0]

            with dve.Fori(0, E // 2) as u:
                for par in range(2):
                    wait_credit(dve, d_y[par], u * 16)
                    for half in range(2):
                        k = 2 * par + half
                        dve.wait_ge(y_full, u * 4 + k + 1)
                        dve.tensor_copy(yb[:, par, 2 * half:2 * half + 2, :],
                                        r_bank[half].rearrange("p (t d) -> p t d", t=2)).then_inc(y_free, 1)
            dve.wait_ge(d_rg, 16 * B)
            for n in range(16):
                dve.wait_ge(d_yg[n], 16)
                dve.scalar_tensor_tensor(out=rg[:, n, :], in0=yg[:, n, :], scalar=wtok[:, n // T, n % T:n % T + 1], in1=rg[:, n, :],
                                         op0=ALU.mult, op1=ALU.add).then_inc(o_ready, 1)
    return nc


def kernel(**inputs):
    import numpy as np
    import concourse.bacc as bacc
    from concourse import mybir as mb
    from concourse.bass_utils import run_bass_kernel_spmd

    f = np.float32

    def get(name):
        return np.asarray(inputs[name])

    consts = np.zeros((P, C_ALL), f)
    i = np.arange(P)
    consts[:, C_ID:C_ID + P] = i[:, None] == i[None, :]
    consts[:, C_PRE:C_PRE + P] = i[:, None] < i[None, :]
    consts[:, C_MQ:C_MQ + P] = np.where(i[None, :] > i[:, None], f(-1e30), f(0))
    consts[:, C_MK:C_MK + P] = np.where(i[:, None] > i[None, :], f(-1e30), f(0))
    consts[:, C_REV:C_REV + E] = E - np.arange(E)
    consts[:, C_JUNK:C_JUNK + T] = SLOTS + np.arange(T)[None, :] * P + i[:, None]
    freqs = f(1.0) / f(10000.0) ** (np.arange(HD // 2, dtype=f) / f(HD // 2))
    angle = (np.arange(S, dtype=f)[:, None] * freqs[None, :]).reshape(T, P, HD // 2).transpose(1, 0, 2)
    consts[:, C_COS:C_COS + T * HD] = np.repeat(np.cos(angle), 2, axis=2).reshape(P, T * HD)
    consts[:, C_SIN:C_SIN + T * HD] = np.stack([-np.sin(angle), np.sin(angle)], axis=3).reshape(P, T * HD)

    bkv = get("L0_xattn_bkv")
    arrays = {
        "x": get("x"),
        "ctxT": get("ctx_768").transpose(0, 2, 1),
        "consts": consts,
        "wqkv": np.concatenate([get("L0_attn_Wq"), get("L0_attn_Wk"), get("L0_attn_Wv")], axis=1),
        "wo": get("L0_attn_Wo"),
        "xwq": get("L0_xattn_Wq"),
        "xwkv": get("L0_xattn_Wkv"),
        "xwo": get("L0_xattn_Wo"),
        "bq": get("L0_xattn_bq").reshape(C, P).T,
        "bk": bkv[0:D].reshape(C, P).T,
        "rows5": np.broadcast_to(np.stack([get("L0_attn_bo"), get("L0_xattn_bo"), bkv[D:2 * D], get("L0_ffn_ln_gamma"),
                                           get("L0_ffn_ln_beta")])[None], (P, 5, D)),
        "gateT": get("L0_ffn_gate_weight").T,
        "wi": get("L0_ffn_wi"),
        "wo_e": get("L0_ffn_wo"),
    }
    arrays = {k: np.ascontiguousarray(a) for k, a in arrays.items()}
    nc = bacc.Bacc("TRN2", target_bir_lowering=False, num_devices=1)
    args = [nc.dram_tensor("in_" + k, a.shape, mb.dt.from_np(a.dtype), kind="ExternalInput").ap() for k, a in arrays.items()]
    args.append(nc.dram_tensor("out_0", (B, S, D), F32, kind="ExternalOutput").ap())
    build(nc, *args)
    r = run_bass_kernel_spmd(nc, [{"in_" + k: a for k, a in arrays.items()}], core_ids=[0])
    return r.results[0]["out_0"]
```

```python
from contextlib import ExitStack

import concourse.bass as bass
from concourse import mybir

P = 128
F32 = mybir.dt.float32
F32R = mybir.dt.float32r
BF16 = mybir.dt.bfloat16
I32 = mybir.dt.int32
ALU = mybir.AluOpType
ACT = mybir.ActivationFunctionType
AX_X = mybir.AxisListType.X

B, S, D = 4, 512, 256
DC = 192
H, HD = 16, 16
E, I, CAP = 8, 1024, 512
N_TOK = B * S
T = S // P
C = D // P
CK = DC // 2
G, GH = 4, 4
IC = I // P
EPS = 1e-5
SCALE = HD ** -0.5
SLOTS = E * CAP

Q_PLACES = (0, 1, 0)
K_PLACES = (1, 2, 2)
PLACE_OF = {"q": (0, 1, 2), "k": (2, 1, 0)}
SROWS = HD * (3 + len(Q_PLACES))
NPB = 3
XROWS = SROWS + 2

C_PRE, C_MQ, C_MK, C_ID, C_REV, C_JUNK, C_COS, C_SIN = 0, 128, 256, 384, 512, 520, 524, 588
C_ALL = C_SIN + T * HD


SEGMENTS = [(a, 2 * pair + p) for pair in range(B // 2) for a in range(2) for p in range(2)]
JOBS = [(a, b, g) for a, b in SEGMENTS for g in range(G)]
SLOTS_OF_JOB = T * GH
AT_MAX, AT_MAX_MOVE = 19, 20
AT_EXP, AT_PV = 27, 31
AT_OT = AT_PV + SLOTS_OF_JOB + 2
AT_NORM = AT_OT + 1
N_SLOTS = SLOTS_OF_JOB * (len(JOBS) - 1) + AT_NORM + 1
N_S, N_E = 3, 2
PARTS_OF = {"lnx": 6, "lny": 6, "fin": 7, "xT": 2, "qk": 4, "v": 2, "rT": 5, "kc": 3, "vc": 2, "oT": 2, "o": 2, "yT": 2,
            "qc": 3, "tT": 2, "logit": 1, "rank": 1}
AHEAD = [(f, n) for f in (("lnx", 0), ("xT", 0), ("qk", 0), ("rT", 0), ("v", 0)) for n in range(PARTS_OF[f[0]])]
FILL = {}


def add_fills():
    def put(step, slot, f, every=1):
        for n in range(PARTS_OF[f[0]]):
            FILL.setdefault(min(step * SLOTS_OF_JOB + slot + n * every, N_SLOTS - 1), []).append((f, n))

    put(0, 6, ("lnx", 1))
    put(0, 13, ("xT", 1), 2)
    put(1, 6, ("qk", 1), 2)
    put(2, 6, ("rT", 1), 2)
    put(3, 6, ("v", 1), 2)
    for s, (a, b) in enumerate(SEGMENTS):
        at = G * s
        if a == 0:
            put(at + 5, 12, ("kc", b), 2)
            put(at + 6, 3, ("oT", b, 0), 1)
            put(at + 6, 6, ("o", b, 0))
            put(at + 6, 8, ("lny", b))
            put(at + 7, 0, ("yT", b), 2)
            put(at + 7, 6, ("qc", b), 2)
            put(at + 7, 13, ("vc", b), 2)
        else:
            if b + 2 < B:
                put(at + 4, 7, ("lnx", b + 2))
                put(at + 4, 14, ("xT", b + 2), 2)
                put(at + 5, 4, ("qk", b + 2), 2)
                put(at + 5, 12, ("rT", b + 2), 2)
                put(at + 6, 8, ("v", b + 2), 2)
            put(at + 6, 11, ("oT", b, 1), 2)
            put(at + 7, 0, ("o", b, 1), 5)
            put(at + 7, 7, ("fin", b))
            put(at + 8, 6, ("tT", b), 2)
            put(at + 8, 10, ("logit", b))
            put(at + 8, 13, ("rank", b))


add_fills()
SPLIT_KINDS = ("rT", "kc", "qc")
NO_BANK = ("lnx", "lny", "fin")
S_USES = ([(h, tiles) for h in range(GH) for tiles in ((3,), (0, 2), (1,))],
          [(h, (q,)) for h in range(GH) for q in range(T)])


def at_slot(slot, stage):
    j, n = divmod(slot - stage, SLOTS_OF_JOB)
    return (JOBS[j], n) if 0 <= j < len(JOBS) else (None, n)


def job_at(slot, stage):
    j, n = at_slot(slot, stage)
    return j if n == 0 else None


def scores_at(slot):
    j, n = at_slot(slot, 0)
    return [(j, k) for k in range(n * len(S_USES[j[0]]) // SLOTS_OF_JOB, (n + 1) * len(S_USES[j[0]]) // SLOTS_OF_JOB)] if j else []


def values_at(slot):
    j, n = at_slot(slot, AT_PV)
    rate = SLOTS_OF_JOB / (SLOTS_OF_JOB - 2)
    return [(j, k) for k in range(int((n - 2) * rate), int((n - 1) * rate))] if j and n >= 2 else []


def walk():
    for f, n in AHEAD:
        yield ("fill", f, n)
    for slot in range(N_SLOTS):
        yield ("slot", slot)
        for f, n in FILL.get(slot, ()):
            yield ("fill", f, n)


class Counts:

    def __init__(self):
        self.ring, self.score, self.exp, self.split, self.norm, self.bias = {}, {}, {}, {}, {}, {}
        for w in walk():
            if w[0] == "fill":
                _, f, n = w
                if f[0] in NO_BANK:
                    if n == 0:
                        self.norm[f] = len(self.norm)
                        if f[0] != "fin":
                            self.bias[f] = len(self.bias)
                elif f[0] not in SPLIT_KINDS:
                    self.ring[f + (n,)] = len(self.ring)
                elif n < PARTS_OF[f[0]] - 1:
                    self.ring[f + (n,)] = len(self.ring)
                    self.split[f + (n,)] = len(self.split)
            else:
                slot = w[1]
                for use in scores_at(slot):
                    self.score[use] = len(self.score)
                j, n = at_slot(slot, AT_EXP)
                if j:
                    self.exp[j, n] = len(self.exp)
                if job_at(slot, AT_MAX):
                    self.ring[("max", job_at(slot, AT_MAX))] = len(self.ring)
                if job_at(slot, AT_OT):
                    self.ring[("ot", job_at(slot, AT_OT))] = len(self.ring)


def build(nc, x, ctxT, consts, wqkv, wo, xwq, xwkv, xwo, bq, bk, rows5, gateT, wi, wo_e, out):
    cnt = Counts()
    spill = nc.dram_tensor("spill", [NPB, P, 3, S], BF16, kind="Internal")
    disp = nc.dram_tensor("disp", [SLOTS + N_TOK, D], F32, kind="Internal")
    ydram = nc.dram_tensor("ydram", [SLOTS, D], F32, kind="Internal")
    resid = nc.dram_tensor("resid", [B, S, D], F32, kind="Internal")

    with ExitStack() as stack:
        def sb(name, shape, dt=F32):
            return stack.enter_context(nc.sbuf_tensor(name, shape, dt))

        def sem(name):
            return stack.enter_context(nc.semaphore(name))

        def two(name):
            return [sem(name + "0"), sem(name + "1")]

        cst = sb("cst", [P, C_ALL - 3 * P])
        cosT = cst[:, C_COS - C_ID:C_COS - C_ID + T * HD].rearrange("p (t d) -> p t d", t=T)
        sinT = cst[:, C_SIN - C_ID:C_SIN - C_ID + T * HD].rearrange("p (t d) -> p t d", t=T)
        identf = cst[:, 0:P]
        cstb = sb("cstb", [P, 4 * P], BF16)
        prefb, maskqb, maskkb, identb = (cstb[:, n * P:(n + 1) * P] for n in range(4))
        onesb = sb("onesb", [P, P], BF16)
        wqkv_sb = sb("wqkv_sb", [P, C, 3 * D])
        wo_sb = [sb("wo_sb", [P, C, D]), sb("xwo_sb", [P, C, D])]
        xwq_sb = sb("xwq_sb", [P, C, D])
        xwkv_sb = sb("xwkv_sb", [CK, 2, 2 * D])
        bq_sb = sb("bq_sb", [P, C])
        bk_sb = sb("bk_sb", [P, C])
        rows_sb = sb("rows_sb", [P, 5, D])
        bo_sb = [rows_sb[:, 0, :], rows_sb[:, 1, :]]
        bv_sb, gam_sb, bet_sb = (rows_sb[:, n, :] for n in (2, 3, 4))
        gate_sb = sb("gate_sb", [P, C, E])

        xn = [sb("xn0", [P, T, D]), sb("xn1", [P, T, D])]
        tok = sb("tok", [P, T, D])
        xnT = sb("xnT", [P, C, S])
        ctx_sb = sb("ctx_sb", [CK, 2, S])
        rs = sb("rs", [P, 2, 2 * D])
        att = sb("att", [P, T, D])
        attT = sb("attT", [P, C, S])
        pv_sb = sb("pv_sb", [P, S])
        cst4 = pv_sb
        rem32 = sb("rem32", [P, 2, S])
        parts = sb("parts", [P, NPB, 3, S], BF16)
        rsum = sb("rsum", [P, 2, T, GH])
        mx = sb("mx", [P, 2, GH, T])
        nmx = sb("nmx", [P, 2, 2, GH * T], BF16)
        mrow = sb("mrow", [2 * GH * T, 2, P], BF16)
        stats = sb("stats", [P, T, 6])
        mv = sb("mv", [P, T, 2])
        scale2 = sb("scale2", [P, T])
        var2 = sb("var2", [P, 2, T])
        guess2 = sb("guess2", [P, 2, T])
        rstd2 = sb("rstd2", [P, 2, T])
        z = sb("z", [P, T, E])
        ez = sb("ez", [P, T, E])
        cand = sb("cand", [P, T, E])
        onehot = sb("onehot", [P, T, E])
        onehotb = sb("onehotb", [P, T, E], BF16)
        rk = sb("rk", [P, T, E])
        count = sb("count", [P, E])
        icount = sb("icount", [P, E], I32)
        small = sb("small", [P, 12, T])
        junk = sb("junk", [P, T])
        sidx = sb("sidx", [P, T], I32)
        gidx = sb("gidx", [P, B, T], I32)
        wtok = sb("wtok", [P, B, T])
        with ExitStack() as attention:
            def sba(name, shape, dt=F32):
                return attention.enter_context(nc.sbuf_tensor(name, shape, dt))

            prob = sba("prob", [P, T, GH, S])
            qst = [sba(f"qst{p}", [P, H, S], BF16) for p in range(2)]
            kst = [sba(f"kst{p}", [P, H, S], BF16) for p in range(2)]
            V = [sba(f"v{p}", [P, T, H, 2 * HD]) for p in range(2)]
            xb = [sba(f"xb{n}", [P, T, D]) for n in range(3)]
            rot = sba("rot", [P, T, 2 * D])
        with ExitStack() as experts:
            def sbe(name, shape, dt=F32):
                return experts.enter_context(nc.sbuf_tensor(name, shape, dt))

            w_raw = sbe("w_raw", [P, 2, 2 * C * I])
            sbe("under_w_hi", [P, 2, 2 * C * I])
            h_all = sbe("h_all", [P, IC, CAP])
            sbe("under_h_hi", [P, IC, CAP])
            dsp = sbe("dsp", [P, 2, T, D])
            yb = sbe("yb", [P, 2, T, D])
        w_lo = sb("w_lo", [P, 2, 2 * C * I], F32R)
        w_hi = sb("w_hi", [P, 2, 2 * C * I], F32R)
        h_lo = sb("h_lo", [P, IC, CAP], F32R)
        h_hi = sb("h_hi", [P, IC, CAP], F32R)
        sb("under_rows", [P, 4, T, D])
        x_hi = sb("x_hi", [P, 2, C, CAP], F32R)
        x_lo = sb("x_lo", [P, 2, C, CAP], F32R)
        yg, rg = (k[:, :, :].rearrange("p h s -> p (h s)").bitcast(F32).rearrange("p (n d) -> p n d", n=B * T) for k in kst)

        def wi_of(w, par):
            return w[:, par, 0:C * I].rearrange("p (c d) -> p c d", c=C)

        def wo_of(w, par):
            return w[:, par, C * I:2 * C * I].rearrange("p (c d) -> p c d", c=IC)

        ps = stack.enter_context(nc.psum_tensor("ps", [P, 8, S], F32))
        s_bank = [ps[:, n, :] for n in range(N_S)]
        e_bank = [ps[:, N_S + n, :] for n in range(N_E)]
        pv_bank = ps[:, 5, :]
        r_bank = [ps[:, n, :] for n in (6, 7)]

        d_cst, d_w, d_ctx, d_out, d_zero = (sem(n) for n in ("d_cst", "d_w", "d_ctx", "d_out", "d_zero"))
        d_wqkv = sem("d_wqkv")
        d_x = [sem(f"d_x{n}") for n in range(3)]
        c_ready, v_ready, z_ready = sem("c_ready"), sem("v_ready"), sem("z_ready")
        ring_full = two("ring_full")
        ring_moved = two("ring_moved")
        xn_ready = sem("xn_ready")
        bias_ready = sem("bias_ready")
        rot_ready = sem("rot_ready")
        hi_ready, mid_ready = sem("hi_ready"), sem("mid_ready")
        rem_ready, lo_ready = sem("rem_ready"), sem("lo_ready")
        d_spill = [sem(f"d_spill{n}") for n in range(NPB)]
        d_q = [[sem(f"d_q{p}{c}") for c in range(C)] for p in range(2)]
        d_k = [[sem(f"d_k{p}{c}") for c in range(C)] for p in range(2)]
        s_full, s_free = sem("s_full"), sem("s_free")
        mx_ready = sem("mx_ready")
        d_max = [[sem(f"d_max{p}{g}") for g in range(G)] for p in range(2)]
        e_full, e_done = sem("e_full"), sem("e_done")
        pv_full, pv_moved = sem("pv_full"), sem("pv_moved")
        res_ready, d_res = sem("res_ready"), two("d_res")
        tokg_ready, tok_ready = sem("tokg_ready"), sem("tok_ready")
        ez_ready, oh_ready = sem("ez_ready"), sem("oh_ready")
        idx_ready, d_scat = sem("idx_ready"), sem("d_scat")
        chain = sem("chain")
        h_hi_ready, count_ready = sem("h_hi_ready"), sem("count_ready")
        w_hi_ready, wi_lo_ready, wo_lo_ready, x_hi_ready, h_split = (sem(n) for n in ("w_hi_ready", "wi_lo_ready", "wo_lo_ready", "x_hi_ready", "h_split"))
        t_full, t_free, h_full, h_free, y_full, y_free = (sem(n) for n in ("t_full", "t_free", "h_full", "h_free", "y_full", "y_free"))
        d_wi, d_wo, d_dsp, d_y = two("d_wi"), two("d_wo"), two("d_dsp"), two("d_y")
        d_rg, d_yg = sem("d_rg"), [sem(f"d_yg{n}") for n in range(16)]
        o_ready = sem("o_ready")

        block = stack.enter_context(nc.Block())

        def wait(eng, s, value):
            if value > 0:
                eng.wait_ge(s, value)

        def wait_credit(eng, s, value):
            eng.wait_ge(s, value + 1)

        def either_width(eng, e, body):
            tokens = eng.value_load(icount[0:1, bass.ds(e, 1)], min_val=0, max_val=N_TOK)
            with eng.If(tokens > CAP // 2):
                body(CAP)
            with eng.Else():
                body(CAP // 2)

        def weights_low(eng, par, n, ready):
            q = slice(n * I, (n + 1) * I)
            eng.tensor_tensor(w_lo[:, par, q], w_raw[:, par, q], w_hi[:, par, q].bitcast(F32), ALU.subtract).then_inc(ready, 1)

        def part(f, n, level):
            k_side = f[0] == "kc" or f[0] == "rT" and n % 2 == 1
            return parts[:, cnt.split[f + (n,)] % NPB, PLACE_OF["k" if k_side else "q"][level], :]

        def full(eng, name):
            n = cnt.ring[name]
            eng.wait_ge(ring_full[n % 2], n // 2 + 1)

        def bank(name):
            return r_bank[cnt.ring[name] % 2]

        def filled(ins, name):
            ins.then_inc(ring_full[cnt.ring[name] % 2], 1)

        def moved(eng, *names):
            for n in (0, 1):
                wait(eng, ring_moved[n], max([cnt.ring[name] // 2 + 1 for name in names if cnt.ring[name] % 2 == n], default=0))

        def ring_uses(n):
            return (len(cnt.ring) + 1 - n) // 2

        def moves(ins, name):
            ins.then_inc(ring_moved[cnt.ring[name] % 2], 1)

        def stack_full(a, b):
            return ((b // 2) * 2 + a + 1) * 16 * (1 + len(Q_PLACES))

        def max_rows_sent(j):
            a, b, g = j
            return ((b // 2) * 2 + a) * 32 + 32

        @block.sync
        def _(sp):
            def stack_places(f):
                p = f[1] % 2
                if f[0] == "rT":
                    return [(qst[p], d_q[p][0], 0, 0), (kst[p], d_k[p][0], 0, 0), (qst[p], d_q[p][1], 1, 0), (kst[p], d_k[p][1], 1, 0)]
                stk, sems = (kst[p], d_k[p]) if f[0] == "kc" else (qst[p], d_q[p])
                return [(stk, sems[c], c, 1) for c in range(C)]

            def load_wi(e, par):
                sp.dma_start(wi_of(w_raw, par), wi[e].rearrange("(c p) n -> p c n", p=P)).then_inc(d_wi[par], 16)

            def load_wo(e, par):
                sp.dma_start(wo_of(w_raw, par), wo_e[e].rearrange("(c p) n -> p c n", p=P)).then_inc(d_wo[par], 16)

            sent = []

            def stack_part(f, n):
                places = stack_places(f)
                if n < len(places):
                    k = cnt.split[f + (n,)]
                    sp.wait_ge(lo_ready, k + 1)
                    if k >= NPB:
                        sp.wait_ge(*sent[k - NPB])
                    sp.dma_start(spill[k % NPB], parts[:, k % NPB, :, :]).then_inc(d_spill[k % NPB], 16)
                if n > 0:
                    k = cnt.split[f + (n - 1,)]
                    stk, done, c, a = places[n - 1]
                    sp.wait_ge(d_spill[k % NPB], 16 * (k // NPB + 1))
                    sp.dma_start(stk[0:3 * HD, 8 * c:8 * c + 8, :], spill[k % NPB].rearrange("(h d) j n -> (d j) h n", h=8)).then_inc(done, 16)
                    for i, j in enumerate(Q_PLACES if stk in qst else K_PLACES):
                        sp.dma_start(stk[(3 + i) * HD:(4 + i) * HD, 8 * c:8 * c + 8, :],
                                     spill[k % NPB, :, j, :].rearrange("(h d) n -> d h n", h=8)).then_inc(done, 16)
                    sent.append((done, stack_full(a, f[1])))

            def max_job(j):
                a, b, g = j
                k = JOBS.index(j)
                moved(sp, ("max", j))
                for part in range(2):
                    sp.dma_start(qst[b % 2][SROWS + part:SROWS + part + 1, GH * g:GH * g + GH, :].rearrange("p h (t c) -> p (h t) c", c=P),
                                 mrow[16 * part:16 * part + 16, k % 2, :]).then_inc(d_max[b % 2][g], 16)

            def load_rows(b):
                sp.dma_start(xb[b % 3][:, :, :], x[b].rearrange("(t p) d -> p t d", p=P)).then_inc(d_x[b % 3], 16)

            def load_ctx(b):
                sp.dma_start(ctx_sb[:, :, :], ctxT[b].rearrange("(c p) n -> p c n", p=CK)).then_inc(d_ctx, 16)

            def fill(f, n):
                kind, b = f[0:2]
                if kind in SPLIT_KINDS:
                    stack_part(f, n)
                if f == ("oT", B - 1, 1) and n == 0:
                    sp.wait_ge(pv_full, len(JOBS))
                    for par in range(2):
                        load_wi(par, par)
                        load_wo(par, par)
                if kind == "vc" and n == 1 and b + 1 < B:
                    full(sp, ("vc", b, 1))
                    load_ctx(b + 1)
                if kind == "fin" and n == PARTS_OF["fin"] - 1:
                    sp.wait_ge(res_ready, b + 1)
                    sp.dma_start(resid[b].rearrange("(t p) d -> p t d", p=P), xn[b % 2][:, :, :]).then_inc(d_res[b % 2], 16)
                    if b + 3 < B:
                        load_rows(b + 3)

            load_rows(0)
            sp.dma_start(cst[:, :], consts[:, C_ID:C_ALL]).then_inc(d_cst, 16)
            sp.dma_start(cst4[:, :], consts[:, 0:4 * P]).then_inc(d_cst, 16)
            sp.dma_start(wqkv_sb[:, :, :], wqkv.rearrange("(c p) n -> p c n", p=P)).then_inc(d_wqkv, 16)
            load_rows(1)
            for dst, src in ((wo_sb[0], wo), (xwq_sb, xwq), (wo_sb[1], xwo), (gate_sb, gateT)):
                sp.dma_start(dst[:, :, :], src.rearrange("(c p) n -> p c n", p=P)).then_inc(d_w, 16)
            sp.dma_start(xwkv_sb[:, :, :], xwkv.rearrange("(c p) n -> p c n", p=CK)).then_inc(d_w, 16)
            sp.dma_start(bq_sb[:, :], bq).then_inc(d_w, 16)
            sp.dma_start(bk_sb[:, :], bk).then_inc(d_w, 16)
            sp.dma_start(rows_sb[:, :, :], rows5).then_inc(d_w, 16)
            load_ctx(0)
            load_rows(2)
            sp.wait_ge(z_ready, 1)
            for n in range(E):
                sp.dma_start(disp[n * CAP:(n + 1) * CAP, :].rearrange("(t p) d -> p t d", p=P),
                             tok[:, :, :]).then_inc(d_zero, 16)
            for w in walk():
                if w[0] == "fill":
                    fill(*w[1:])
                elif job_at(w[1], AT_MAX_MOVE):
                    max_job(job_at(w[1], AT_MAX_MOVE))

            def load_slots(e, par):
                sp.dma_start(dsp[:, par, :, :], disp[bass.ds(e * CAP, CAP), :].rearrange("(t p) d -> p t d", p=P)).then_inc(d_dsp[par], 16)

            for n in (0, 1):
                sp.wait_ge(ring_full[n], ring_uses(n))
            sp.wait_ge(d_scat, B * T * 16)
            for par in range(2):
                load_slots(par, par)
            sp.wait_ge(t_full, C)
            load_slots(2, 0)
            with sp.Fori(0, E // 2) as u:
                for par in range(2):
                    sp.wait_ge(h_full, u * (2 * IC) + (par + 1) * IC)
                    load_wi((u * 2 + (par + 2)) % E, par)
                    sp.wait_ge(t_full, u * (2 * C) + (par + 2) * C)
                    load_slots((u * 2 + (par + 3)) % E, 1 - par)
                    sp.wait_ge(y_full, u * 4 + 2 * par + 2)
                    load_wo((u * 2 + (par + 2)) % E, par)
                    wait_credit(sp, y_free, u * 4 + 2 * par + 2)
                    sp.dma_start(ydram[bass.ds(u * (2 * CAP) + par * CAP, CAP), :].rearrange("(t p) d -> p t d", p=P),
                                 yb[:, par, :, :]).then_inc(d_y[par], 16)
            for par in range(2):
                wait_credit(sp, d_y[par], 8 * E)
            for b in range(B):
                sp.dma_start(rg[:, 4 * b:4 * b + 4, :], resid[b].rearrange("(t p) d -> p t d", p=P)).then_inc(d_rg, 16)
            for b in range(B):
                sp.wait_ge(o_ready, 4 * b + 4)
                sp.dma_start(out[b].rearrange("(t p) d -> p t d", p=P), rg[:, 4 * b:4 * b + 4, :]).then_inc(d_out, 16)
            sp.wait_ge(d_out, 16 * B)
            for par in range(2):
                sp.wait_ge(d_wi[par], 8 * E + 16)
                sp.wait_ge(d_wo[par], 8 * E + 16)
                sp.wait_ge(d_dsp[par], 8 * E + (32, 16)[par])

        @block.gpsimd
        def _(pool):
            pool.memset(onesb[:, :], 1.0).then_inc(c_ready, 1)
            pool.memset(count[:, :], 0.0).then_inc(c_ready, 1)
            pool.memset(tok[:, :, :], 0.0).then_inc(z_ready, 1)
            for v in V:
                pool.memset(v[:, :, :, HD:2 * HD], 1.0).then_inc(v_ready, 1)
            pool.wait_ge(v_ready, 2)
            pool.memset(kst[0][SROWS:XROWS, :, :], 1.0).then_inc(v_ready, 1)
            pool.wait_ge(v_ready, 3)
            pool.memset(kst[1][SROWS:XROWS, :, :], 1.0).then_inc(v_ready, 1)
            pool.wait_ge(v_ready, 4)

            def add_bias(a, b):
                f = ("lnx", "lny")[a], b
                pool.wait_ge(xn_ready, (cnt.norm[f] + 1) * T)
                pool.wait_ge(d_w, 16 * 8)
                for t in range(T):
                    ins = pool.tensor_tensor(xb[b % 3][:, t, :], xb[b % 3][:, t, :], bo_sb[a], ALU.add)
                ins.then_inc(bias_ready, 1)

            def fill(f, n):
                kind, b = f[0:2]
                if kind == "lnx" and n == 5:
                    add_bias(0, b)
                if kind == "lny" and n == 5:
                    add_bias(1, b)
                if kind == "qk":
                    moved(pool, f + (n,))
                    pool.tensor_tensor(rot[:, n, :], rot[:, n, :], rs[:, n % 2, :], ALU.add).then_inc(rot_ready, 1)
                if kind in SPLIT_KINDS and n > 0:
                    k = cnt.split[f + (n - 1,)]
                    pool.wait_ge(mid_ready, k + 1)
                    pool.tensor_tensor(part(f, n - 1, 2), rem32[:, k % 2, :], part(f, n - 1, 1), ALU.subtract).then_inc(lo_ready, 1)
                if f == ("fin", B - 1) and n == 0:
                    for k in (0, 1):
                        pool.wait_ge(w_hi_ready, k + 1)
                        weights_low(pool, 0, k, wi_lo_ready)
                if kind == "fin" and n == 6:
                    for t in range(T):
                        pool.wait_ge(tokg_ready, b * T + t + 1)
                        pool.tensor_tensor(tok[:, t, :], tok[:, t, :], bet_sb, ALU.add).then_inc(tok_ready, 1)
                    pool.tensor_tensor(xn[b % 2][:, :, :], xn[b % 2][:, :, :], xb[b % 3][:, :, :], ALU.add).then_inc(res_ready, 1)
                if kind == "rank":
                    pool.wait_ge(idx_ready, b + 1)
                    pool.wait_ge(d_zero, 16 * E)
                    for t in range(T):
                        pool.indirect_dma_start(disp[:, :], bass.IndirectOffsetOnAxis(ap=sidx[:, t:t + 1], axis=0),
                                                tok[:, t, :], None).then_inc(d_scat, 16)

            for w in walk():
                if w[0] == "fill":
                    fill(*w[1:])
            with pool.Fori(0, E // 2) as u:
                for par in range(2):
                    for k in (0, 1):
                        pool.wait_ge(w_hi_ready, u * 8 + par * 4 + 5 + k)
                        weights_low(pool, 1 - par, k, wi_lo_ready)
            for par in range(2):
                wait_credit(pool, d_y[par], 8 * E)
            for n in range(16):
                pool.indirect_dma_start(yg[:, n, :], None, ydram[:, :],
                                        bass.IndirectOffsetOnAxis(ap=gidx[:, n // T, n % T:n % T + 1], axis=0)).then_inc(d_yg[n], 16)

        @block.scalar
        def _(act):
            def move(name, dst, func=ACT.Copy, src=None, **kw):
                full(act, name)
                moves(act.activation(dst, bank(name) if src is None else src, func, **kw), name)

            def exp(j, m):
                kt, h = divmod(m, GH)
                q0 = kt * P if j[0] == 0 else 0
                n = cnt.exp[j, m]
                act.wait_ge(e_full, n + 1)
                act.activation(prob[:, kt, h, q0:S], e_bank[n % N_E][:, q0:S], ACT.Exp, scale=SCALE).then_inc(e_done, 1)

            def split(f, n):
                bias = {"kc": bk_sb, "qc": bq_sb}.get(f[0])
                if bias is not None:
                    act.wait_ge(d_w, 16 * 8)
                if n < PARTS_OF[f[0]] - 1:
                    k = cnt.split[f + (n,)]
                    wait(act, d_spill[k % NPB], 16 * (k // NPB))
                    full(act, f + (n,))
                    if bias is None:
                        ins = act.activation(part(f, n, 0), bank(f + (n,)), ACT.Copy)
                    else:
                        ins = act.activation(part(f, n, 0), bank(f + (n,)), ACT.Identity, bias=bias[:, n:n + 1])
                    ins.then_inc(hi_ready, 1)
                if n > 0:
                    k = cnt.split[f + (n - 1,)]
                    moved(act, f + (n - 1,))
                    act.activation(part(f, n - 1, 1), rem32[:, k % 2, :], ACT.Copy).then_inc(mid_ready, 1)

            def weights_high(par, n):
                q = slice(n * I, (n + 1) * I)
                act.activation(w_hi[:, par, q], w_raw[:, par, q], ACT.Copy).then_inc(w_hi_ready, 1)

            def fill(f, n):
                kind, b = f[0:2]
                if f == ("fin", B - 1) and n == 0:
                    act.wait_ge(d_wi[0], 16)
                    act.wait_ge(d_wo[0], 16)
                    for k in range(4):
                        weights_high(0, k)
                if kind in ("xT", "yT", "tT"):
                    move(f + (n,), xnT[:, n, :])
                if kind == "oT":
                    move(f + (n,), attT[:, n, :])
                if kind == "v":
                    name = f + (n,)
                    move(name, V[b % 2][:, 2 * n:2 * n + 2, :, 0:HD], src=bank(name).rearrange("p (t h d) -> p t h d", t=2, h=H))
                if kind in SPLIT_KINDS:
                    split(f, n)
                if kind == "logit":
                    moved(act, f + (0,))
                    act.activation(ez[:, :, :], z[:, :, :], ACT.Exp).then_inc(ez_ready, 1)

            for w in walk():
                if w[0] == "fill":
                    fill(*w[1:])
                else:
                    slot = w[1]
                    if job_at(slot, AT_PV + SLOTS_OF_JOB):
                        j = job_at(slot, AT_PV + SLOTS_OF_JOB)
                        act.wait_ge(pv_full, JOBS.index(j) + 1)
                        if JOBS.index(j) > 0:
                            full(act, ("ot", JOBS[JOBS.index(j) - 1]))
                        act.activation(pv_sb[:, :], pv_bank, ACT.Copy).then_inc(pv_moved, 1)
                    j, n = at_slot(slot, AT_EXP)
                    if j:
                        exp(j, n)
            def slots_high(par):
                for c in range(C):
                    act.activation(x_hi[:, par, c, :], ps[:, c, :], ACT.Copy).then_inc(x_hi_ready, 1)

            act.wait_ge(t_full, C)
            slots_high(0)
            act.wait_ge(count_ready, 1)
            with act.Fori(0, E // 2) as u:
                for par in range(2):
                    def hidden(width):
                        for n in range(IC):
                            act.wait_ge(h_full, u * (2 * IC) + par * IC + n + 1)
                            act.activation(h_all[:, n, 0:width], ps[:, 2 + n % 4, 0:width], ACT.Gelu).then_inc(h_free, 1)
                            if n in (IC // 2 - 1, IC - 1):
                                act.wait_ge(d_wi[1 - par], (u + par) * 16 + 16)
                                weights_high(1 - par, n // (IC // 2))

                    either_width(act, u * 2 + par, hidden)
                    act.wait_ge(t_full, u * (2 * C) + (par + 2) * C)
                    slots_high(1 - par)
                    act.wait_ge(d_wo[1 - par], (u + par) * 16 + 16)
                    for k in (2, 3):
                        weights_high(1 - par, k)

        @block.tensor
        def _(pe):
            def take(name, *reads):
                for n in (0, 1):
                    counts = [cnt.ring[r] // 2 + 1 for r in reads if cnt.ring[r] % 2 == n]
                    counts += [cnt.ring[name] // 2] * (cnt.ring[name] % 2 == n)
                    wait(pe, ring_moved[n], max(counts, default=0))
                return bank(name)

            def turn(name, src, ready=None, value=None, reads=()):
                dst = take(name, *reads)
                for t in range(T):
                    if ready is not None:
                        pe.wait_ge(ready, value + t + 1)
                    mm = pe.transpose(dst[:, t * P:(t + 1) * P], src(t), identf)
                filled(mm, name)

            def product(dst, n_chunks, lhsT, rhs):
                for c in range(n_chunks):
                    mm = pe.matmul(dst, lhsT(c), rhs(c), start=(c == 0), stop=(c == n_chunks - 1))
                return mm

            def score(j, n):
                a, b, g = j
                p = b % 2
                hh, tiles = S_USES[a][n]
                h = GH * g + hh
                k = cnt.score[j, n]
                wait(pe, s_free, k - N_S + 1)
                dst, o = s_bank[k % N_S], 0
                for qt in tiles:
                    w = (qt + 1) * P if a == 0 else S
                    mm = pe.matmul(dst[:, o:o + w], qst[p][0:SROWS, h, qt * P:(qt + 1) * P], kst[p][0:SROWS, h, 0:w],
                                   start=True, stop=True)
                    if a == 0:
                        mm = pe.matmul(dst[:, o + w - P:o + w], identb, maskqb, start=False, stop=True, skip_group_check=True)
                    o += w
                mm.then_inc(s_full, 1)

            def score_T(j, m):
                a, b, g = j
                kt, hh = divmod(m, GH)
                h, p = GH * g + hh, b % 2
                n = cnt.exp[j, m]
                if m == 0:
                    pe.wait_ge(v_ready, 4)
                    pe.wait_ge(d_max[p][g], max_rows_sent(j))
                wait(pe, e_done, n - N_E + 1)
                q0 = kt * P if a == 0 else 0
                dst = e_bank[n % N_E]
                mm = pe.matmul(dst[:, q0:S], kst[p][0:XROWS, h, kt * P:(kt + 1) * P], qst[p][0:XROWS, h, q0:S], start=True, stop=True)
                if a == 0:
                    mm = pe.matmul(dst[:, q0:q0 + P], identb, maskkb, start=False, stop=True, skip_group_check=True)
                mm.then_inc(e_full, 1)

            def values(j, m):
                a, b, g = j
                kt, hh = divmod(m, GH)
                if m == 0:
                    wait(pe, pv_moved, JOBS.index(j))
                    if g == 0:
                        moved(pe, *(((("v", b, n) if a == 0 else ("vc", b, n)) for n in range(2))))
                pe.wait_ge(e_done, cnt.exp[j, m] + 1)
                q0 = kt * P if a == 0 else 0
                mm = pe.matmul(pv_bank[32 * hh:32 * hh + 32, q0:S], V[b % 2][:, kt, GH * g + hh, :], prob[:, kt, hh, q0:S],
                               start=(kt == 0), stop=True, skip_group_check=True)
                if m == SLOTS_OF_JOB - 1:
                    mm.then_inc(pv_full, 1)

            def turn_max(j):
                name = ("max", j)
                k = JOBS.index(j)
                dst = take(name).bitcast(BF16)
                pe.wait_ge(mx_ready, k + 1)
                filled(pe.transpose(dst[0:2 * GH * T, 0:P], nmx[:, k % 2, :, :].rearrange("p j n -> p (j n)"), identb), name)

            def slot_work(slot):
                for j, n in scores_at(slot):
                    a, b, g = j
                    if n == 0 and g % 2 == 0:
                        for d in (d_q, d_k):
                            pe.wait_ge(d[b % 2][g // 2], stack_full(a, b))
                    score(j, n)
                for j, m in values_at(slot):
                    values(j, m)
                j, m = at_slot(slot, AT_EXP)
                if j:
                    score_T(j, m)
                if job_at(slot, AT_MAX):
                    turn_max(job_at(slot, AT_MAX))
                if job_at(slot, AT_OT):
                    j = job_at(slot, AT_OT)
                    pe.wait_ge(pv_moved, JOBS.index(j) + 1)
                    turn(("ot", j), lambda t: pv_sb[:, t * P:(t + 1) * P])

            def fill(f, n):
                kind, b = f[0:2]
                p = b % 2
                if kind in ("xT", "yT"):
                    turn(f + (n,), lambda t: xn[p][:, t, n * P:(n + 1) * P], xn_ready, T * cnt.norm["lnx" if kind == "xT" else "lny", b])
                if kind == "tT":
                    turn(f + (n,), lambda t: tok[:, t, n * P:(n + 1) * P], tok_ready, b * T)
                if kind == "oT":
                    turn(f + (n,), lambda t: att[:, t, n * P:(n + 1) * P], reads=(("ot", (f[2], b, G - 1)),))
                if kind == "qk":
                    pe.wait_ge(d_wqkv, 16)
                    dst = take(f + (n,), ("xT", b, 0), ("xT", b, 1))
                    filled(product(dst, C, lambda c: xnT[:, c, n * P:(n + 1) * P], lambda c: wqkv_sb[:, c, 0:2 * D]), f + (n,))
                if kind == "rT" and n < 4:
                    j = (0, 2, 1, 3)[n]
                    turn(f + (n,), lambda t: rot[:, t, j * P:(j + 1) * P], rot_ready, b * T)
                if kind == "kc" and n < C:
                    pe.wait_ge(d_ctx, 16 * b + 16)
                    pe.wait_ge(d_w, 16 * 8)
                    dst = take(f + (n,))
                    filled(product(dst, 2, lambda c: xwkv_sb[:, c, n * P:(n + 1) * P], lambda c: ctx_sb[:, c, :]), f + (n,))
                if kind == "qc" and n < C:
                    dst = take(f + (n,), ("yT", b, 0), ("yT", b, 1))
                    filled(product(dst, C, lambda c: xwq_sb[:, c, n * P:(n + 1) * P], lambda c: xnT[:, c, :]), f + (n,))
                if kind in ("v", "vc", "o"):
                    chunks, lhs, rhs, reads = {
                        "v": (C, xnT, wqkv_sb[:, :, 2 * D:3 * D], ()),
                        "vc": (2, ctx_sb, xwkv_sb[:, :, D:2 * D], ()),
                        "o": (C, attT, wo_sb[f[-1] % 2], (("oT",) + f[1:] + (0,), ("oT",) + f[1:] + (1,))),
                    }[kind]
                    dst = take(f + (n,), *reads)
                    for i in range(2):
                        t = 2 * n + i
                        mm = product(dst[:, i * D:(i + 1) * D], chunks, lambda c: lhs[:, c, t * P:(t + 1) * P], lambda c: rhs[:, c, :])
                    filled(mm, f + (n,))
                if kind == "logit":
                    dst = take(f + (0,), ("tT", b, 0), ("tT", b, 1))
                    for t in range(T):
                        mm = product(dst[:, t * E:(t + 1) * E], C, lambda c: xnT[:, c, t * P:(t + 1) * P], lambda c: gate_sb[:, c, :])
                    filled(mm, f + (0,))
                if kind == "rank":
                    dst = take(f + (0,))
                    pe.wait_ge(oh_ready, b + 1)
                    oh = onehotb[:, :, :].rearrange("p t e -> p (t e)")
                    pe.matmul(dst[:, 0:T * E], prefb, oh, start=True, stop=True, skip_group_check=True)
                    for k in range(1, T):
                        pe.matmul(dst[:, k * E:T * E], onesb[:, :], oh[:, 0:(T - k) * E], start=False, stop=True, skip_group_check=True)
                    for t in range(T):
                        mm = pe.matmul(dst[:, T * E:(T + 1) * E], onesb[:, :], oh[:, t * E:(t + 1) * E], start=False,
                                       stop=True, skip_group_check=True)
                    filled(mm, f + (0,))

            for s in (h_free, y_free):
                pe.sem_inc(s, 1)
            pe.wait_ge(d_cst, 32)
            pe.wait_ge(c_ready, 4)
            for w in walk():
                if w[0] == "fill":
                    fill(*w[1:])
                else:
                    slot_work(w[1])

            def turn_slots(par, loads, used):
                pe.wait_ge(d_dsp[par], loads)
                for c in range(C):
                    if used is not None:
                        pe.wait_ge(t_free, used + c)
                    for t in range(T):
                        mm = pe.transpose(ps[:, c, :][:, t * P:(t + 1) * P], dsp[:, par, t, c * P:(c + 1) * P], identf)
                    mm.then_inc(t_full, 1)

            pe.wait_ge(s_free, len(cnt.score))
            turn_slots(0, 16, None)
            pe.wait_ge(e_done, len(cnt.exp))
            for n in (0, 1):
                pe.wait_ge(ring_moved[n], ring_uses(n))

            def product3(dst, chunks, lhsT_hi, lhsT_lo, rhs_hi, rhs_lo):
                k = 0
                for c in range(chunks):
                    for lhsT, rhs in ((lhsT_hi, rhs_hi), (lhsT_hi, rhs_lo), (lhsT_lo, rhs_hi)):
                        k += 1
                        mm = pe.matmul(dst, lhsT(c), rhs(c), start=(k == 1), stop=(k == 3 * chunks))
                return mm

            pe.wait_ge(count_ready, 1)
            with pe.Fori(0, E // 2) as u:
                for par in range(2):
                    def expert(width):
                        for n in range(IC):
                            k = par * IC + n
                            wait_credit(pe, h_free, u * (2 * IC) + max(k - 3, 0))
                            product3(ps[:, 2 + n % 4, 0:width], C,
                                     lambda c: wi_of(w_hi, par)[:, c, n * P:(n + 1) * P], lambda c: wi_of(w_lo, par)[:, c, n * P:(n + 1) * P],
                                     lambda c: x_hi[:, par, c, 0:width], lambda c: x_lo[:, par, c, 0:width]).then_inc(h_full, 1)
                        turn_slots(1 - par, (u + par) * 16 + 16, u * 4 + 2 * par + 1)
                        pe.wait_ge(wo_lo_ready, u * 4 + par * 2 + 2)
                        pe.wait_ge(h_split, u * (2 * IC) + (par + 1) * IC)
                        for half in range(2):
                            k = 2 * par + half
                            wait_credit(pe, y_free, u * 4 + max(k - 1, 0))
                            if half * (CAP // 2) >= width:
                                continue
                            for i in range(2):
                                t = 2 * half + i
                                mm = product3(r_bank[half][:, i * D:(i + 1) * D], IC,
                                              lambda n: h_hi[:, n, t * P:(t + 1) * P], lambda n: h_lo[:, n, t * P:(t + 1) * P],
                                              lambda n: wo_of(w_hi, par)[:, n, :], lambda n: wo_of(w_lo, par)[:, n, :])
                            mm.then_inc(y_full, CAP // width)

                    pe.wait_ge(t_free, u * 4 + 2 * par + 2)
                    pe.wait_ge(wi_lo_ready, u * 4 + par * 2 + 2)
                    either_width(pe, u * 2 + par, expert)

        @block.vector
        def _(dve):
            links = [0]

            def link(ins):
                links[0] += 1
                ins.then_inc(chain, 1)
                dve.wait_ge(chain, links[0])

            def rsqrt_start(twice):
                k = slice(0, 2 if twice else 1)
                v, guess, dst = var2[:, k, :], guess2[:, k, :], rstd2[:, k, :]
                link(dve.tensor_scalar(var2[:, 0, :], mv[:, :, 1], EPS, None, ALU.add))
                if twice:
                    link(dve.scalar_tensor_tensor(out=var2[:, 1, :], in0=var2[:, 0, :], scalar=EPS, in1=mv[:, :, 1],
                                                  op0=ALU.mult, op1=ALU.add))
                link(dve.tensor_scalar(guess.bitcast(I32), v.bitcast(I32), 1, None, ALU.logical_shift_right))
                link(dve.tensor_scalar(dst.bitcast(I32), guess.bitcast(I32), -1.0, float(0x5f3759df), ALU.mult, ALU.add))
                newton_step(twice)

            def newton_step(twice):
                k = slice(0, 2 if twice else 1)
                v, guess, dst = var2[:, k, :], guess2[:, k, :], rstd2[:, k, :]
                link(dve.tensor_tensor(guess, dst, dst, ALU.mult))
                link(dve.scalar_tensor_tensor(out=guess, in0=guess, scalar=-0.5, in1=v, op0=ALU.mult, op1=ALU.mult))
                link(dve.scalar_tensor_tensor(out=dst, in0=guess, scalar=1.5, in1=dst, op0=ALU.add, op1=ALU.mult))

            def norm_part(f, n):
                b = f[1]
                if n in (0, 1):
                    for t in (2 * n, 2 * n + 1):
                        i = dve.bn_stats(stats[:, t, :], xb[b % 3][:, t, :])
                    link(i)
                if n == 2:
                    for t in range(T):
                        i = dve.bn_aggr(mv[:, t, :], stats[:, t, :])
                    link(i)
                    rsqrt_start(f[0] == "fin")
                if n == 3:
                    newton_step(f[0] == "fin")
                    newton_step(f[0] == "fin")
                if n in (4, 5):
                    for t in (2 * n - 8, 2 * n - 7):
                        dve.tensor_scalar(xn[b % 2][:, t, :], xb[b % 3][:, t, :], mv[:, t, 0:1], rstd2[:, 0, t:t + 1],
                                          ALU.subtract, ALU.mult).then_inc(xn_ready, 1)

            def rope(f, t):
                name = f + (t,)
                full(dve, name)
                if t >= 2:
                    dve.wait_ge(rot_ready, f[1] * T + t - 1)
                src = bank(name).rearrange("p (h d) -> p h d", d=HD)
                pr = src.rearrange("p h (i two) -> p h i two", two=2)
                o = rs[:, t % 2, :].rearrange("p (h i two) -> p h i two", h=2 * H, two=2)
                sn = sinT[:, t, :].rearrange("p (i two) -> p i two", two=2)
                dve.tensor_tensor(rot[:, t, :].rearrange("p (h d) -> p h d", d=HD), src,
                                  cosT[:, t:t + 1, :].to_broadcast([P, 2 * H, HD]), ALU.mult)
                for k in range(2):
                    i = dve.tensor_tensor(o[:, :, :, k], pr[:, :, :, 1 - k],
                                          sn[:, :, k:k + 1].rearrange("p i o -> p o i").to_broadcast([P, 2 * H, HD // 2]),
                                          ALU.mult)
                moves(i, name)

            def split(f, n):
                k = cnt.split[f + (n,)]
                bias = {"kc": bk_sb, "qc": bq_sb}.get(f[0])
                dve.wait_ge(hi_ready, k + 1)
                wait(dve, lo_ready, k - 1)
                if bias is None:
                    ins = dve.tensor_tensor(rem32[:, k % 2, :], bank(f + (n,)), part(f, n, 0), ALU.subtract)
                else:
                    ins = dve.scalar_tensor_tensor(out=rem32[:, k % 2, :], in0=bank(f + (n,)), scalar=bias[:, n:n + 1],
                                                   in1=part(f, n, 0), op0=ALU.add, op1=ALU.subtract)
                moves(ins, f + (n,))

            def maxima(j, n):
                a, b, g = j
                hh, tiles = S_USES[a][n]
                k = cnt.score[j, n]
                dve.wait_ge(s_full, k + 1)
                o = 0
                for qt in tiles:
                    w = (qt + 1) * P if a == 0 else S
                    i = dve.tensor_reduce(mx[:, JOBS.index(j) % 2, hh, qt:qt + 1], s_bank[k % N_S][:, o:o + w], AX_X, ALU.max)
                    o += w
                i.then_inc(s_free, 1)

            def negate(j):
                par = JOBS.index(j) % 2
                dve.wait_ge(s_free, cnt.score[j, len(S_USES[j[0]]) - 1] + 1)
                m = mx[:, par, :, :].rearrange("p h t -> p (h t)")
                link(dve.tensor_scalar(nmx[:, par, 0, :], m, -1.0, None, ALU.mult))
                dve.scalar_tensor_tensor(out=nmx[:, par, 1, :], in0=m, scalar=-1.0, in1=nmx[:, par, 0, :],
                                         op0=ALU.mult, op1=ALU.subtract).then_inc(mx_ready, 1)

            def max_rows(j):
                k = JOBS.index(j)
                full(dve, ("max", j))
                if k >= 2:
                    a, b, g = JOBS[k - 2]
                    dve.wait_ge(d_max[b % 2][g], max_rows_sent(JOBS[k - 2]))
                moves(dve.tensor_copy(mrow[:, k % 2, :], bank(("max", j)).bitcast(BF16)[0:2 * GH * T, 0:P]), ("max", j))

            def normalise(j):
                a, b, g = j
                k = JOBS.index(j) % 2
                full(dve, ("ot", j))
                src = bank(("ot", j)).rearrange("p (t h d) -> p t h d", t=T, h=GH)
                link(dve.reciprocal(rsum[:, k, :, :], src[:, :, :, HD:HD + 1].rearrange("p t h o -> p t (h o)")))
                for t in range(T):
                    i = dve.tensor_tensor(att[:, t, g * GH * HD:(g + 1) * GH * HD].rearrange("p (h d) -> p h d", h=GH), src[:, t, :, 0:HD],
                                          rsum[:, k, t, :].rearrange("p (h o) -> p h o", o=1).to_broadcast([P, GH, HD]), ALU.mult)
                moves(i, ("ot", j))

            def route_logits(f):
                full(dve, f + (0,))
                logit = bank(f + (0,))[:, 0:T * E].rearrange("p (t e) -> p t e", t=T)
                link(dve.tensor_reduce(col(TOP), logit, AX_X, ALU.max))
                moves(dve.tensor_tensor(z[:, :, :], logit, wide(TOP), ALU.subtract), f + (0,))
                moved(dve, f + (0,))
                link(dve.scalar_tensor_tensor(out=cand[:, :, :], in0=z[:, :, :], scalar=0.0, in1=rev, op0=ALU.is_ge, op1=ALU.mult))
                link(dve.tensor_reduce(col(LAST), cand[:, :, :], AX_X, ALU.max))
                link(dve.tensor_tensor(onehot[:, :, :], rev, wide(LAST), ALU.is_equal))
                dve.tensor_copy(onehotb[:, :, :], onehot[:, :, :]).then_inc(oh_ready, 1)
                dve.wait_ge(ez_ready, f[1] + 1)
                link(dve.tensor_reduce(col(DEN), ez[:, :, :], AX_X, ALU.add))
                link(dve.reciprocal(col(PROB), col(DEN)))

            def col(k):
                return small[:, k, :]

            def wide(k):
                return small[:, k, :].rearrange("p (t o) -> p t o", o=1).to_broadcast([P, T, E])

            rev = cst[:, C_REV - C_ID:C_REV - C_ID + E].rearrange("p (o e) -> p o e", o=1).to_broadcast([P, T, E])
            TOP, LAST, DEN, PROB, RANK, KEEP, BASE, KRANK, DIFF, PICK = range(10)

            def route_ranks(f):
                b = f[1]
                full(dve, f + (0,))
                pr = bank(f + (0,))
                link(dve.tensor_tensor(rk[:, :, :], pr[:, 0:T * E].rearrange("p (t e) -> p t e", t=T),
                                          count[:, :].rearrange("p (o e) -> p o e", o=1).to_broadcast([P, T, E]), ALU.add))
                moves(dve.tensor_tensor(count[:, :], pr[:, T * E:(T + 1) * E], count[:, :], ALU.add), f + (0,))
                link(dve.tensor_tensor(rk[:, :, :], rk[:, :, :], onehot[:, :, :], ALU.mult))
                link(dve.tensor_reduce(col(RANK), rk[:, :, :], AX_X, ALU.add))
                dve.tensor_scalar(col(KEEP), col(RANK), float(CAP), None, ALU.is_lt)
                link(dve.tensor_scalar(col(BASE), col(LAST), -float(CAP), float(SLOTS), ALU.mult, ALU.add))
                link(dve.tensor_tensor(col(KRANK), col(KEEP), col(RANK), ALU.mult))
                dve.tensor_tensor(wtok[:, b, :], col(PROB), col(KEEP), ALU.mult)
                link(dve.tensor_tensor(col(KRANK), col(BASE), col(KRANK), ALU.add))
                dve.tensor_copy(gidx[:, b, :], col(KRANK))
                link(dve.tensor_tensor(col(DIFF), col(KRANK), junk[:, :], ALU.subtract))
                link(dve.tensor_tensor(col(PICK), col(DIFF), col(KEEP), ALU.mult))
                dve.tensor_tensor(sidx[:, :], col(PICK), junk[:, :], ALU.add).then_inc(idx_ready, 1)
                link(dve.tensor_scalar(junk[:, :], junk[:, :], float(S), None, ALU.add))
                if b == B - 1:
                    dve.tensor_copy(icount[:, :], count[:, :]).then_inc(count_ready, 1)
                moved(dve, f + (0,))

            def fill(f, n):
                kind, b = f[0:2]
                if kind == "lnx" and n == 0:
                    dve.wait_ge(d_x[b % 3], 16 * (b // 3) + 16)
                if kind == "lny" and n == 4:
                    wait(dve, d_res[b % 2], 16 * (b // 2))
                if kind in ("lnx", "lny"):
                    norm_part(f, n)
                if kind == "qk":
                    rope(f, n)
                if kind == "kc":
                    dve.wait_ge(d_w, 16 * 8)
                if kind in SPLIT_KINDS and n < PARTS_OF[kind] - 1:
                    split(f, n)
                if kind == "vc":
                    full(dve, f + (n,))
                    src = bank(f + (n,)).rearrange("p (t h d) -> p t h d", t=2, h=H)
                    for i in range(2):
                        ins = dve.tensor_tensor(V[b % 2][:, 2 * n + i, :, 0:HD], src[:, i, :, :],
                                                bv_sb.rearrange("p (h d) -> p h d", h=H), ALU.add)
                    moves(ins, f + (n,))
                if kind == "o":
                    dve.wait_ge(bias_ready, cnt.bias[("lnx", "lny")[f[2]], b] + 1)
                    full(dve, f + (n,))
                    rows = xb[b % 3][:, 2 * n:2 * n + 2, :]
                    moves(dve.tensor_tensor(rows, bank(f + (n,)).rearrange("p (t d) -> p t d", t=2), rows, ALU.add), f + (n,))
                    moved(dve, f + (n,))
                if kind == "fin" and n < 6:
                    norm_part(f, n)
                    if n == 3:
                        link(dve.tensor_tensor(scale2[:, :], var2[:, 0, :], rstd2[:, 0, :], ALU.mult))
                        link(dve.tensor_tensor(scale2[:, :], scale2[:, :], rstd2[:, 1, :], ALU.mult))
                if kind == "fin" and n == 6:
                    dve.wait_ge(d_w, 16 * 8)
                    if b == 0:
                        dve.wait_ge(d_zero, 16 * E)
                    dve.wait_ge(xn_ready, (cnt.norm[f] + 1) * T)
                    wait(dve, d_scat, b * (16 * T))
                    for t in range(T):
                        dve.scalar_tensor_tensor(out=tok[:, t, :], in0=xn[b % 2][:, t, :], scalar=scale2[:, t:t + 1], in1=gam_sb,
                                                 op0=ALU.mult, op1=ALU.mult).then_inc(tokg_ready, 1)
                if kind == "logit":
                    route_logits(f)
                if kind == "rank":
                    route_ranks(f)

            for s in d_y:
                dve.sem_inc(s, 1)
            dve.wait_ge(d_cst, 32)
            dve.tensor_copy(cstb[:, :], cst4[:, :]).then_inc(c_ready, 1)
            dve.tensor_copy(junk[:, :], cst[:, C_JUNK - C_ID:C_JUNK - C_ID + T]).then_inc(c_ready, 1)
            dve.wait_ge(c_ready, 4)
            for w in walk():
                if w[0] == "fill":
                    fill(*w[1:])
                else:
                    slot = w[1]
                    for j, n in scores_at(slot):
                        maxima(j, n)
                        if n == len(S_USES[j[0]]) - 1:
                            negate(j)
                    if job_at(slot, AT_MAX_MOVE):
                        max_rows(job_at(slot, AT_MAX_MOVE))
                    if job_at(slot, AT_NORM):
                        normalise(job_at(slot, AT_NORM))

            def slots_low(par, c):
                dve.tensor_tensor(x_lo[:, par, c, :], ps[:, c, :], x_hi[:, par, c, :].bitcast(F32), ALU.subtract).then_inc(t_free, 1)

            for k in (2, 3):
                dve.wait_ge(w_hi_ready, k + 1)
                weights_low(dve, 0, k, wo_lo_ready)
            dve.wait_ge(count_ready, 1)
            for c in range(C):
                dve.wait_ge(x_hi_ready, c + 1)
                slots_low(0, c)
            with dve.Fori(0, E // 2) as u:
                for par in range(2):
                    def hidden_parts(width):
                        for n in range(IC):
                            w = slice(0, width)
                            wait_credit(dve, h_free, u * (2 * IC) + par * IC + n + 1)
                            dve.tensor_copy(h_hi[:, n, w], h_all[:, n, w]).then_inc(h_hi_ready, 1)
                            dve.wait_ge(h_hi_ready, u * (2 * IC) + par * IC + n + 1)
                            dve.tensor_tensor(h_lo[:, n, w], h_all[:, n, w], h_hi[:, n, w].bitcast(F32), ALU.subtract).then_inc(h_split, 1)

                    either_width(dve, u * 2 + par, hidden_parts)
                    for c in range(C):
                        dve.wait_ge(x_hi_ready, u * (2 * C) + (par + 1) * C + c + 1)
                        slots_low(1 - par, c)
                    for k in (2, 3):
                        dve.wait_ge(w_hi_ready, u * 8 + par * 4 + 5 + k)
                        weights_low(dve, 1 - par, k, wo_lo_ready)
                    wait_credit(dve, d_y[par], u * 16)
                    for half in range(2):
                        k = 2 * par + half
                        dve.wait_ge(y_full, u * 4 + k + 1)
                        dve.tensor_copy(yb[:, par, 2 * half:2 * half + 2, :],
                                        r_bank[half].rearrange("p (t d) -> p t d", t=2)).then_inc(y_free, 1)
            dve.wait_ge(d_rg, 16 * B)
            for n in range(16):
                dve.wait_ge(d_yg[n], 16)
                dve.scalar_tensor_tensor(out=rg[:, n, :], in0=yg[:, n, :], scalar=wtok[:, n // T, n % T:n % T + 1], in1=rg[:, n, :],
                                         op0=ALU.mult, op1=ALU.add).then_inc(o_ready, 1)
    return nc


def kernel(**inputs):
    import numpy as np
    import concourse.bacc as bacc
    from concourse import mybir as mb
    from concourse.bass_utils import run_bass_kernel_spmd

    f = np.float32

    def get(name):
        return np.asarray(inputs[name])

    consts = np.zeros((P, C_ALL), f)
    i = np.arange(P)
    consts[:, C_ID:C_ID + P] = i[:, None] == i[None, :]
    consts[:, C_PRE:C_PRE + P] = i[:, None] < i[None, :]
    consts[:, C_MQ:C_MQ + P] = np.where(i[None, :] > i[:, None], f(-1e30), f(0))
    consts[:, C_MK:C_MK + P] = np.where(i[:, None] > i[None, :], f(-1e30), f(0))
    consts[:, C_REV:C_REV + E] = E - np.arange(E)
    consts[:, C_JUNK:C_JUNK + T] = SLOTS + np.arange(T)[None, :] * P + i[:, None]
    freqs = f(1.0) / f(10000.0) ** (np.arange(HD // 2, dtype=f) / f(HD // 2))
    angle = (np.arange(S, dtype=f)[:, None] * freqs[None, :]).reshape(T, P, HD // 2).transpose(1, 0, 2)
    consts[:, C_COS:C_COS + T * HD] = np.repeat(np.cos(angle), 2, axis=2).reshape(P, T * HD)
    consts[:, C_SIN:C_SIN + T * HD] = np.stack([-np.sin(angle), np.sin(angle)], axis=3).reshape(P, T * HD)

    bkv = get("L0_xattn_bkv")
    arrays = {
        "x": get("x"),
        "ctxT": get("ctx_768").transpose(0, 2, 1),
        "consts": consts,
        "wqkv": np.concatenate([get("L0_attn_Wq"), get("L0_attn_Wk"), get("L0_attn_Wv")], axis=1),
        "wo": get("L0_attn_Wo"),
        "xwq": get("L0_xattn_Wq"),
        "xwkv": get("L0_xattn_Wkv"),
        "xwo": get("L0_xattn_Wo"),
        "bq": get("L0_xattn_bq").reshape(C, P).T,
        "bk": bkv[0:D].reshape(C, P).T,
        "rows5": np.broadcast_to(np.stack([get("L0_attn_bo"), get("L0_xattn_bo"), bkv[D:2 * D], get("L0_ffn_ln_gamma"),
                                           get("L0_ffn_ln_beta")])[None], (P, 5, D)),
        "gateT": get("L0_ffn_gate_weight").T,
        "wi": get("L0_ffn_wi"),
        "wo_e": get("L0_ffn_wo"),
    }
    arrays = {k: np.ascontiguousarray(a) for k, a in arrays.items()}
    nc = bacc.Bacc("TRN2", target_bir_lowering=False, num_devices=1)
    args = [nc.dram_tensor("in_" + k, a.shape, mb.dt.from_np(a.dtype), kind="ExternalInput").ap() for k, a in arrays.items()]
    args.append(nc.dram_tensor("out_0", (B, S, D), F32, kind="ExternalOutput").ap())
    build(nc, *args)
    r = run_bass_kernel_spmd(nc, [{"in_" + k: a for k, a in arrays.items()}], core_ids=[0])
    return r.results[0]["out_0"]
```
